# Optimizing a Trainium2 kernel written in Bass

```python
import numpy as np
import jax
import jax.numpy as jnp

def _softmax(x, axis=-1):
    return jax.nn.softmax(x, axis=axis)

def _gelu(x):
    return jax.nn.gelu(x, approximate=True)

def _silu(x):
    return jax.nn.silu(x)

def _sigmoid(x):
    return jax.nn.sigmoid(x)

def _layernorm(x, axis=-1, eps=1e-05):
    m = jnp.mean(x, axis=axis, keepdims=True)
    v = jnp.var(x, axis=axis, keepdims=True)
    return (x - m) / jnp.sqrt(v + eps)

def _scatter_add(tgt, idx, src, axis=0):
    return tgt.at[idx].add(src)

def _segment_sum(src, seg, n):
    return jax.ops.segment_sum(src, seg, n)
kernel_name = 'mk_hybrid_d1_jaxref_r4_53d7ef'

def setup_inputs(seed: int=0):
    np.random.seed(seed)
    _w = jnp.asarray

    def _L0_attn_a_setup():
        import jax, jax.numpy as jnp
        import numpy as np
        L, H, D_MODEL, FFN = (2, 8, 256, 1024)
        HD = D_MODEL // H
        SCALE_BASE = 128
        EPS = 1e-05

        def _layernorm(x, w, b):
            mu = x.mean(-1, keepdims=True)
            var = ((x - mu) ** 2).mean(-1, keepdims=True)
            return (x - mu) * jax.lax.rsqrt(var + EPS) * w + b

        def _groupnorm(y, w, b):
            B, S, _ = y.shape
            yg = y.reshape(B, S, H, HD)
            mu = yg.mean(-1, keepdims=True)
            var = ((yg - mu) ** 2).mean(-1, keepdims=True)
            yn = ((yg - mu) * jax.lax.rsqrt(var + EPS)).reshape(B, S, H * HD)
            return yn * w + b

        def _xpos_tables(S):
            scale_vec = (np.arange(0, HD, 2) + 0.4 * HD) / (1.4 * HD)
            power = (np.arange(S, dtype=np.float64) / SCALE_BASE)[:, None]
            scale = scale_vec[None, :] ** power
            half = HD // 2
            inv_freq = 1.0 / 10000.0 ** (np.arange(half, dtype=np.float64) / half)
            ang = np.arange(S, dtype=np.float64)[:, None] * inv_freq[None, :]
            sin, cos = (np.sin(ang), np.cos(ang))
            dup = lambda m: jnp.asarray(np.repeat(m, 2, axis=-1).astype(np.float32))
            return (dup(sin * scale), dup(cos * scale), dup(sin / scale), dup(cos / scale))

        def _rotate_every_two(x):
            x1, x2 = (x[..., ::2], x[..., 1::2])
            return jnp.stack((-x2, x1), axis=-1).reshape(x.shape)

        def _decay_mask(S):
            gammas = 1.0 - np.exp(np.linspace(np.log(1.0 / 32), np.log(1.0 / 128), H))
            n = np.arange(S)[:, None]
            m = np.arange(S)[None, :]
            diff = (n - m).astype(np.float64)
            D = np.where(n >= m, gammas[:, None, None] ** diff[None], 0.0)
            return jnp.asarray(D.astype(np.float32))
        key = jax.random.key(seed)
        ks = jax.random.split(key, 8)
        B, S = (2, 512)
        rn = lambda k, shape, s: jax.random.normal(k, shape, dtype=jnp.float32) * s
        return {'X': rn(ks[0], (B, S, D_MODEL), 1.0), 'ln1_w': jnp.ones((L, D_MODEL), jnp.float32), 'ln1_b': jnp.zeros((L, D_MODEL), jnp.float32), 'ln2_w': jnp.ones((L, D_MODEL), jnp.float32), 'ln2_b': jnp.zeros((L, D_MODEL), jnp.float32), 'WQ': rn(ks[1], (L, H, D_MODEL, HD), 1.0 / D_MODEL), 'WK': rn(ks[2], (L, H, D_MODEL, HD), 1.0 / D_MODEL), 'WV': rn(ks[3], (L, H, D_MODEL, HD), 1.0 / D_MODEL), 'gn_w': jnp.ones((L, D_MODEL), jnp.float32), 'gn_b': jnp.zeros((L, D_MODEL), jnp.float32), 'WG': rn(ks[4], (L, D_MODEL, D_MODEL), 1.0 / D_MODEL), 'WO': rn(ks[5], (L, D_MODEL, D_MODEL), 1.0 / D_MODEL), 'ffn_w1': rn(ks[6], (L, D_MODEL, FFN), 1.0 / np.sqrt(D_MODEL)), 'ffn_b1': jnp.zeros((L, FFN), jnp.float32), 'ffn_w2': rn(ks[7], (L, FFN, D_MODEL), 1.0 / np.sqrt(FFN)), 'ffn_b2': jnp.zeros((L, D_MODEL), jnp.float32)}
    _L0_attn_a_in = _L0_attn_a_setup()

    def _L0_attn_b_setup():
        import jax, jax.numpy as jnp
        import numpy as np
        import math
        B, S, DIM = (2, 512, 256)
        H, KVH = (16, 4)
        HD = DIM // H
        WINDOW = 64
        ROPE_BASE = 10000.0
        EPS = 1e-06

        def _rms_norm(v):
            return v * jax.lax.rsqrt(jnp.mean(v * v, axis=-1, keepdims=True) + EPS)

        def _rope_tables(seqlen, dtype):
            inv_freq = 1.0 / ROPE_BASE ** (jnp.arange(0, HD, 2, dtype=jnp.float32) / HD)
            t = jnp.arange(seqlen, dtype=jnp.float32)
            freqs = jnp.outer(t, inv_freq)
            return (jnp.cos(freqs).astype(dtype)[None, None], jnp.sin(freqs).astype(dtype)[None, None])

        def _apply_rotary(v, cos, sin):
            half = v.shape[-1] // 2
            v1, v2 = (v[..., :half], v[..., half:])
            return jnp.concatenate((v1 * cos + v2 * sin, -v1 * sin + v2 * cos), axis=-1)
        key = jax.random.key(seed)
        ks = jax.random.split(key, 6)
        s = 0.02
        return {'x': jax.random.normal(ks[0], (B, S, DIM), jnp.float32), 'Wq': jax.random.normal(ks[1], (DIM, DIM), jnp.float32) * s, 'Wk': jax.random.normal(ks[2], (KVH * HD, DIM), jnp.float32) * s, 'Wv': jax.random.normal(ks[3], (KVH * HD, DIM), jnp.float32) * s, 'Wo': jax.random.normal(ks[4], (DIM, DIM), jnp.float32) * s, 'q_gain': jnp.ones((H,), jnp.float32), 'pair_mix': jnp.tile(jnp.eye(2, dtype=jnp.float32), (H // 2, 1, 1)) + 0.01 * jax.random.normal(ks[5], (H // 2, 2, 2), jnp.float32)}
    _L0_attn_b_in = _L0_attn_b_setup()

    def _L0_ffn_setup():
        import jax, jax.numpy as jnp
        import numpy as np
        EPS = 1e-08

        def _ternary_linear(x, w):
            alpha = jnp.mean(jnp.abs(w))
            w_t = jnp.sign(w) * (jnp.abs(w) > 0.5 * alpha).astype(w.dtype)
            w_q = w + jax.lax.stop_gradient(w_t - w)
            d = x.shape[-1]
            rms = jnp.sqrt(jnp.sum(x * x, axis=-1, keepdims=True)) / jnp.sqrt(jnp.asarray(d, x.dtype))
            x_norm = x / (rms + EPS)
            return jnp.einsum('bsd,fd->bsf', x_norm, w_q)
        key = jax.random.key(seed)
        k1, k2, k3 = jax.random.split(key, 3)
        d_model, d_ff = (256, 1024)
        B, S = (4, 1024)
        x = jax.random.normal(k1, (B, S, d_model), dtype=jnp.float32)
        w_up = jax.random.normal(k2, (d_ff, d_model), dtype=jnp.float32) * 0.02
        w_down = jax.random.normal(k3, (d_model, d_ff), dtype=jnp.float32) * 0.02
        return {'x': x, 'w_up': w_up, 'w_down': w_down}
    _L0_ffn_in = _L0_ffn_setup()
    _d = {'L0_attn_a_X': _L0_attn_a_in['X'], 'L0_attn_a_ln1_w': _L0_attn_a_in['ln1_w'], 'L0_attn_a_ln1_b': _L0_attn_a_in['ln1_b'], 'L0_attn_a_ln2_w': _L0_attn_a_in['ln2_w'], 'L0_attn_a_ln2_b': _L0_attn_a_in['ln2_b'], 'L0_attn_a_WQ': _L0_attn_a_in['WQ'], 'L0_attn_a_WK': _L0_attn_a_in['WK'], 'L0_attn_a_WV': _L0_attn_a_in['WV'], 'L0_attn_a_gn_w': _L0_attn_a_in['gn_w'], 'L0_attn_a_gn_b': _L0_attn_a_in['gn_b'], 'L0_attn_a_WG': _L0_attn_a_in['WG'], 'L0_attn_a_WO': _L0_attn_a_in['WO'], 'L0_attn_a_ffn_w1': _L0_attn_a_in['ffn_w1'], 'L0_attn_a_ffn_b1': _L0_attn_a_in['ffn_b1'], 'L0_attn_a_ffn_w2': _L0_attn_a_in['ffn_w2'], 'L0_attn_a_ffn_b2': _L0_attn_a_in['ffn_b2'], 'L0_attn_b_Wq': _L0_attn_b_in['Wq'], 'L0_attn_b_Wk': _L0_attn_b_in['Wk'], 'L0_attn_b_Wv': _L0_attn_b_in['Wv'], 'L0_attn_b_Wo': _L0_attn_b_in['Wo'], 'L0_attn_b_q_gain': _L0_attn_b_in['q_gain'], 'L0_attn_b_pair_mix': _L0_attn_b_in['pair_mix'], 'L0_ffn_w_up': _L0_ffn_in['w_up'], 'L0_ffn_w_down': _L0_ffn_in['w_down']}
    _x0 = _d['L0_attn_a_X']
    _d['L0_attn_a_X'] = jax.random.normal(jax.random.fold_in(jax.random.key(seed), 1), (2, 2048, 256), dtype=_x0.dtype)
    del _x0
    return _d

def reference(L0_attn_a_X, L0_attn_a_ln1_w, L0_attn_a_ln1_b, L0_attn_a_ln2_w, L0_attn_a_ln2_b, L0_attn_a_WQ, L0_attn_a_WK, L0_attn_a_WV, L0_attn_a_gn_w, L0_attn_a_gn_b, L0_attn_a_WG, L0_attn_a_WO, L0_attn_a_ffn_w1, L0_attn_a_ffn_b1, L0_attn_a_ffn_w2, L0_attn_a_ffn_b2, L0_attn_b_Wq, L0_attn_b_Wk, L0_attn_b_Wv, L0_attn_b_Wo, L0_attn_b_q_gain, L0_attn_b_pair_mix, L0_ffn_w_up, L0_ffn_w_down):

    def _L0_attn_a_ref(X, ln1_w, ln1_b, ln2_w, ln2_b, WQ, WK, WV, gn_w, gn_b, WG, WO, ffn_w1, ffn_b1, ffn_w2, ffn_b2):
        import jax, jax.numpy as jnp
        import numpy as np
        L, H, D_MODEL, FFN = (2, 8, 256, 1024)
        HD = D_MODEL // H
        SCALE_BASE = 128
        EPS = 1e-05

        def _layernorm(x, w, b):
            mu = x.mean(-1, keepdims=True)
            var = ((x - mu) ** 2).mean(-1, keepdims=True)
            return (x - mu) * jax.lax.rsqrt(var + EPS) * w + b

        def _groupnorm(y, w, b):
            B, S, _ = y.shape
            yg = y.reshape(B, S, H, HD)
            mu = yg.mean(-1, keepdims=True)
            var = ((yg - mu) ** 2).mean(-1, keepdims=True)
            yn = ((yg - mu) * jax.lax.rsqrt(var + EPS)).reshape(B, S, H * HD)
            return yn * w + b

        def _xpos_tables(S):
            scale_vec = (np.arange(0, HD, 2) + 0.4 * HD) / (1.4 * HD)
            power = (np.arange(S, dtype=np.float64) / SCALE_BASE)[:, None]
            scale = scale_vec[None, :] ** power
            half = HD // 2
            inv_freq = 1.0 / 10000.0 ** (np.arange(half, dtype=np.float64) / half)
            ang = np.arange(S, dtype=np.float64)[:, None] * inv_freq[None, :]
            sin, cos = (np.sin(ang), np.cos(ang))
            dup = lambda m: jnp.asarray(np.repeat(m, 2, axis=-1).astype(np.float32))
            return (dup(sin * scale), dup(cos * scale), dup(sin / scale), dup(cos / scale))

        def _rotate_every_two(x):
            x1, x2 = (x[..., ::2], x[..., 1::2])
            return jnp.stack((-x2, x1), axis=-1).reshape(x.shape)

        def _decay_mask(S):
            gammas = 1.0 - np.exp(np.linspace(np.log(1.0 / 32), np.log(1.0 / 128), H))
            n = np.arange(S)[:, None]
            m = np.arange(S)[None, :]
            diff = (n - m).astype(np.float64)
            D = np.where(n >= m, gammas[:, None, None] ** diff[None], 0.0)
            return jnp.asarray(D.astype(np.float32))
        B, S, _ = X.shape
        sinq, cosq, sink, cosk = _xpos_tables(S)
        Dm = _decay_mask(S)
        for i in range(L):
            Xn = _layernorm(X, ln1_w[i], ln1_b[i])
            Q = jnp.einsum('bsd,hdk->bhsk', Xn, WQ[i])
            K = jnp.einsum('bsd,hdk->bhsk', Xn, WK[i])
            V = jnp.einsum('bsd,hdk->bhsk', Xn, WV[i])
            Q = Q * cosq + _rotate_every_two(Q) * sinq
            K = K * cosk + _rotate_every_two(K) * sink
            scores = jnp.einsum('bhsk,bhtk->bhst', Q, K) * Dm[None]
            Yh = jnp.einsum('bhst,bhtk->bhsk', scores, V)
            Y = Yh.transpose(0, 2, 1, 3).reshape(B, S, H * HD)
            Y = _groupnorm(Y, gn_w[i], gn_b[i])
            G = jax.nn.silu(Xn @ WG[i])
            Y = G * Y @ WO[i] + X
            Yn = _layernorm(Y, ln2_w[i], ln2_b[i])
            X = jax.nn.silu(Yn @ ffn_w1[i] + ffn_b1[i]) @ ffn_w2[i] + ffn_b2[i] + Y
        return X

    def _L0_attn_b_ref(x, Wq, Wk, Wv, Wo, q_gain, pair_mix):
        import jax, jax.numpy as jnp
        import numpy as np
        import math
        B, S, DIM = (2, 512, 256)
        H, KVH = (16, 4)
        HD = DIM // H
        WINDOW = 64
        ROPE_BASE = 10000.0
        EPS = 1e-06

        def _rms_norm(v):
            return v * jax.lax.rsqrt(jnp.mean(v * v, axis=-1, keepdims=True) + EPS)

        def _rope_tables(seqlen, dtype):
            inv_freq = 1.0 / ROPE_BASE ** (jnp.arange(0, HD, 2, dtype=jnp.float32) / HD)
            t = jnp.arange(seqlen, dtype=jnp.float32)
            freqs = jnp.outer(t, inv_freq)
            return (jnp.cos(freqs).astype(dtype)[None, None], jnp.sin(freqs).astype(dtype)[None, None])

        def _apply_rotary(v, cos, sin):
            half = v.shape[-1] // 2
            v1, v2 = (v[..., :half], v[..., half:])
            return jnp.concatenate((v1 * cos + v2 * sin, -v1 * sin + v2 * cos), axis=-1)
        bsz, seqlen, dim = x.shape
        q = (x @ Wq.T).reshape(bsz, seqlen, H, HD).transpose(0, 2, 1, 3)
        k = (x @ Wk.T).reshape(bsz, seqlen, KVH, HD).transpose(0, 2, 1, 3)
        v = (x @ Wv.T).reshape(bsz, seqlen, KVH, HD).transpose(0, 2, 1, 3)
        q = _rms_norm(q)
        k = _rms_norm(k)
        cos, sin = _rope_tables(seqlen, q.dtype)
        q = _apply_rotary(q, cos, sin)
        k = _apply_rotary(k, cos, sin)
        q = q * q_gain.astype(q.dtype)[None, :, None, None]
        rep = H // KVH
        k_full = jnp.repeat(k, rep, axis=1)
        v_full = jnp.repeat(v, rep, axis=1)
        pos = jnp.arange(seqlen)
        mask = (pos[:, None] >= pos[None, :]) & (pos[:, None] - pos[None, :] < WINDOW)
        scale = 1.0 / math.sqrt(HD)
        scores = jnp.einsum('bhqd,bhkd->bhqk', q, k_full) * scale
        scores = jnp.where(mask[None, None], scores, jnp.finfo(scores.dtype).min)
        att = jax.nn.softmax(scores, axis=-1)
        y = jnp.einsum('bhqk,bhkd->bhqd', att, v_full)
        yp = y.reshape(bsz, H // 2, 2, seqlen, HD)
        y = jnp.einsum('bpitd,poi->bpotd', yp, pair_mix.astype(y.dtype)).reshape(bsz, H, seqlen, HD)
        out = y.transpose(0, 2, 1, 3).reshape(bsz, seqlen, dim) @ Wo.T
        return out

    def _L0_ffn_ref(x, w_up, w_down):
        import jax, jax.numpy as jnp
        import numpy as np
        EPS = 1e-08

        def _ternary_linear(x, w):
            alpha = jnp.mean(jnp.abs(w))
            w_t = jnp.sign(w) * (jnp.abs(w) > 0.5 * alpha).astype(w.dtype)
            w_q = w + jax.lax.stop_gradient(w_t - w)
            d = x.shape[-1]
            rms = jnp.sqrt(jnp.sum(x * x, axis=-1, keepdims=True)) / jnp.sqrt(jnp.asarray(d, x.dtype))
            x_norm = x / (rms + EPS)
            return jnp.einsum('bsd,fd->bsf', x_norm, w_q)
        h = jax.nn.gelu(_ternary_linear(x, w_up), approximate=False)
        return _ternary_linear(h, w_down)
    x = L0_attn_a_X
    x = x + _L0_attn_a_ref(_layernorm(x, axis=-1), L0_attn_a_ln1_w, L0_attn_a_ln1_b, L0_attn_a_ln2_w, L0_attn_a_ln2_b, L0_attn_a_WQ, L0_attn_a_WK, L0_attn_a_WV, L0_attn_a_gn_w, L0_attn_a_gn_b, L0_attn_a_WG, L0_attn_a_WO, L0_attn_a_ffn_w1, L0_attn_a_ffn_b1, L0_attn_a_ffn_w2, L0_attn_a_ffn_b2)
    x = x + _L0_ffn_ref(_layernorm(x, axis=-1), L0_ffn_w_up, L0_ffn_w_down)
    x = x + _L0_attn_b_ref(_layernorm(x, axis=-1), L0_attn_b_Wq, L0_attn_b_Wk, L0_attn_b_Wv, L0_attn_b_Wo, L0_attn_b_q_gain, L0_attn_b_pair_mix)
    x = x + _L0_ffn_ref(_layernorm(x, axis=-1), L0_ffn_w_up, L0_ffn_w_down)
    return x

_drawn_inputs = setup_inputs


def setup_inputs(seed=0):
    import zlib

    import numpy as np

    out = dict(_drawn_inputs(seed))
    spreads = {'L0_attn_a_ln1_w': (1.0, 0.6),
     'L0_attn_a_ln1_b': (0.0, 0.8),
     'L0_attn_a_ln2_w': (1.0, 0.2),
     'L0_attn_a_ln2_b': (0.0, 0.1),
     'L0_attn_a_gn_w': (1.0, 0.6),
     'L0_attn_a_gn_b': (0.0, 0.8),
     'L0_attn_a_ffn_b1': (0.0, 0.1),
     'L0_attn_a_ffn_b2': (0.0, 0.1),
     'L0_attn_b_q_gain': (1.0, 0.6)}
    factors = {'L0_attn_a_WQ': 8.0,
     'L0_attn_a_WK': 8.0,
     'L0_attn_a_WV': 8.0,
     'L0_attn_a_WG': 8.0,
     'L0_attn_a_WO': 8.0,
     'L0_attn_b_Wq': 8.0,
     'L0_attn_b_Wk': 8.0,
     'L0_attn_b_Wv': 8.0,
     'L0_attn_b_Wo': 8.0,
     'L0_attn_b_pair_mix': 8.0}
    for name, (base, spread) in spreads.items():
        noise = np.random.default_rng([zlib.crc32(name.encode()), seed]).standard_normal(out[name].shape)
        drawn = base * np.exp(spread * noise) if base else spread * noise
        out[name] = jnp.asarray(drawn.astype(out[name].dtype))
    for name, factor in factors.items():
        out[name] = (out[name] * factor).astype(out[name].dtype)
    return out
```

```python
from contextlib import ExitStack

import numpy as np

import concourse.bass as bass
from concourse import mybir

F32 = mybir.dt.float32
F32R = mybir.dt.float32r
BF16 = mybir.dt.bfloat16
ALU = mybir.AluOpType
ACT = mybir.ActivationFunctionType
AX = mybir.AxisListType

P = 128
D = 256
KD = D // P
FF = 1024
MF = FF // P
B, S = 2, 2048
L = 2
T = B * S
NT = T // P
TB = 4
NB = NT // TB
BT = TB * P
EPS = 1e-5


def at_least(eng, sem, value):
    if isinstance(value, int) and value <= 0:
        return
    eng.wait_ge(sem, value)


def apart(eng, waited):
    eng.sem_inc(waited, 1)


def skewed(eng, body, n, first=1):
    for i in range(first):
        body(i)
    with eng.Fori(first, n) as i:
        body(i)
    body(n)


def prefetch(eng, loads, loaded):
    for tile, dram in loads:
        eng.dma_start(tile, dram).then_inc(loaded, 16)


def live(idx, total):
    return not isinstance(idx, int) or 0 <= idx < total


def input_norm(nc, X, x_dram, loads):
    with ExitStack() as c:
        stats = c.enter_context(nc.sbuf_tensor("n0_stats", [P, NT, 6], F32))
        mv = c.enter_context(nc.sbuf_tensor("n0_mean_var", [P, NT, 2], F32))
        half = c.enter_context(nc.sbuf_tensor("n0_minus_half", [P, NT], F32))
        rstd = c.enter_context(nc.sbuf_tensor("n0_rstd", [P, NT], F32))
        loaded = [nc.alloc_semaphore(f"n0_loaded{b}") for b in range(NB)]
        stats_done = nc.alloc_semaphore("n0_stats_done")
        mv_done = nc.alloc_semaphore("n0_mv_done")
        half_set = nc.alloc_semaphore("n0_half_set")
        eps_added = nc.alloc_semaphore("n0_eps_added")
        rstd_done = nc.alloc_semaphore("n0_rstd_done")
        prefetched = nc.alloc_semaphore("n0_prefetched")
        block = c.enter_context(nc.Block())

        @block.scalar
        def _(act):
            prefetch(act, loads, prefetched)
            act.wait_ge(prefetched, 16 * len(loads))

        @block.sync
        def _(sp):
            for b in range(NB):
                sp.dma_start(X[:, TB * b:TB * b + TB, :],
                             x_dram[BT * b:BT * (b + 1), :].rearrange("(t p) d -> p t d", p=P)
                             ).then_inc(loaded[b], 16)

        def normalise(dve, b):
            dve.wait_ge(rstd_done, b + 1)
            for t in range(TB * b, TB * b + TB):
                nc.vector.tensor_scalar(X[:, t, :], X[:, t, :], mv[:, t, 0:1], rstd[:, t:t + 1],
                                        ALU.subtract, ALU.mult)

        @block.vector
        def _(dve):
            for b in range(NB):
                dve.wait_ge(loaded[b], 16)
                for t in range(TB * b, TB * b + TB):
                    nc.vector.bn_stats(stats[:, t, :], X[:, t, :]).then_inc(stats_done, 1)
                for t in range(TB * b, TB * b + TB):
                    dve.wait_ge(stats_done, t + 1)
                    nc.vector.bn_aggr(mv[:, t, :], stats[:, t, :]).then_inc(mv_done, 1)
                if b >= 1:
                    normalise(dve, b - 1)
            normalise(dve, NB - 1)

        @block.gpsimd
        def _(pool):
            nc.gpsimd.memset(half[:, :], -0.5).then_inc(half_set, 1)
            for b in range(NB):
                ts = slice(TB * b, TB * b + TB)
                pool.wait_ge(mv_done, TB * (b + 1))
                nc.gpsimd.tensor_scalar(rstd[:, ts], mv[:, ts, 1], EPS, None, ALU.add).then_inc(eps_added, 1)
                pool.wait_ge(eps_added, b + 1)
                if b == 0:
                    pool.wait_ge(half_set, 1)
                nc.gpsimd.tensor_tensor(rstd[:, ts], rstd[:, ts], half[:, ts], ALU.pow).then_inc(rstd_done, 1)


def high_halves(nc, jobs, hi_done):
    for stage, _, hi, _ in jobs:
        nc.scalar.activation(hi[:, :, :], stage, ACT.Copy).then_inc(hi_done, 1)


def low_halves(nc, dve, jobs, hi_done, lo_done=None):
    for j, (stage, _, hi, lo) in enumerate(jobs):
        dve.wait_ge(hi_done, j + 1)
        last = nc.vector.tensor_tensor(lo[:, :, :], stage, hi[:, :, :].bitcast(F32), ALU.subtract)
        if lo_done is not None:
            last.then_inc(lo_done, 1)


def at_start(idx):
    return isinstance(idx, int) and idx == 0


def ternary_weights(nc, name, jobs):
    with ExitStack() as c:
        below = c.enter_context(nc.sbuf_tensor(f"{name}_below", [P, P * 16], F32))
        sums = c.enter_context(nc.sbuf_tensor(f"{name}_sums", [P, len(jobs)], F32))
        limit = c.enter_context(nc.sbuf_tensor(f"{name}_limit", [P, 2 * len(jobs)], F32))
        ones = c.enter_context(nc.sbuf_tensor(f"{name}_ones", [P, P], F32))
        total = c.enter_context(nc.psum_tensor(f"{name}_total", [P, 512], F32))
        ones_set, sums_done, total_done, limit_done, below_done, out_done = (
            nc.alloc_semaphore(f"{name}_{s}")
            for s in ("ones_set", "sums_done", "total_done", "limit_done", "below_done", "out_done"))
        block = c.enter_context(nc.Block())

        @block.gpsimd
        def _(pool):
            nc.gpsimd.memset(ones[:, :], 1.0).then_inc(ones_set, 1)

        @block.scalar
        def _(act):
            for j in range(len(jobs)):
                if j:
                    act.wait_ge(sums_done, j)
                nc.scalar.activation(below[:, :], jobs[j][0].rearrange("p k n -> p (k n)"), ACT.Abs,
                                     accum_out=sums[:, j:j + 1]).then_inc(sums_done, 1)

        @block.tensor
        def _(pe):
            pe.wait_ge(ones_set, 1)
            pe.wait_ge(sums_done, len(jobs))
            nc.tensor.matmul(total[:, 0:len(jobs)], ones[:, :], sums[:, :], start=True, stop=True
                             ).then_inc(total_done, 1)

        @block.vector
        def _(dve):
            dve.wait_ge(total_done, 1)
            n = len(jobs)
            count = float(FF * D)
            nc.vector.tensor_scalar(limit[:, 0:n], total[:, 0:n], 1.0 / count, 0.5, ALU.mult, ALU.mult)
            nc.vector.tensor_scalar(limit[:, n:2 * n], total[:, 0:n], 1.0 / count, -0.5, ALU.mult, ALU.mult
                                    ).then_inc(limit_done, 1)
            dve.wait_ge(limit_done, 1)
            for j, (_, out) in enumerate(jobs):
                w = jobs[j][0].rearrange("p k n -> p (k n)")
                if j:
                    dve.wait_ge(out_done, j)
                nc.vector.tensor_scalar(below[:, :], w, limit[:, n + j:n + j + 1], None, ALU.is_lt
                                        ).then_inc(below_done, 1)
                dve.wait_ge(below_done, j + 1)
                nc.vector.scalar_tensor_tensor(out=out[:, :, :].rearrange("p k n -> p (k n)"), in0=w,
                                               scalar=limit[:, j:j + 1], in1=below[:, :],
                                               op0=ALU.is_gt, op1=ALU.subtract).then_inc(out_done, 1)


def ffn(nc, name, X, ident, *, up, down, norm=None, hidden_bias=None, out_bias=None,
        first_input=None, out_dram=None, loads=(), jobs=()):
    ternary = norm is None
    with ExitStack() as c:
        def sb(n, shape, dt=F32):
            return c.enter_context(nc.sbuf_tensor(f"{name}_{n}", shape, dt))

        def sem(n):
            return nc.alloc_semaphore(f"{name}_{n}")

        stats = sb("stats", [P, TB, 6])
        mv = sb("mean_var", [P, 2, TB, 2])
        scale = sb("scale", [P, 2, TB])
        work = sb("scale_work", [P, 3, TB])
        powers = sb("powers", [P, 3, TB])
        xn = sb("xn", [P, 2, TB, D])
        xt = sb("xt", [P, 2, BT])
        xt_hi = sb("xt_hi", [P, 2, KD, BT], F32R)
        xt_lo = sb("xt_lo", [P, 2, KD, BT], F32R)
        h = sb("h", [P, 4, BT])
        h_hi = sb("h_hi", [P, 2, MF, BT], F32R)
        h_lo = sb("h_lo", [P, 2, MF, BT], F32R)
        if ternary:
            h_sq = sb("h_sq", [P, 2, MF, BT])
            ones = sb("ones", [P, 1])
            ms = sb("mean_square", [P, TB])
            rms = sb("rms", [P, 2, TB])
            inv_rms = sb("inv_rms", [P, 2, TB])
        if first_input is not None:
            x_in = sb("x_in", [P, 2, TB, D])
        tp = [c.enter_context(nc.psum_tensor(f"{name}_tp{k}", [P, BT], F32)) for k in range(KD)]
        hp = [c.enter_context(nc.psum_tensor(f"{name}_hp{k}", [P, BT], F32)) for k in range(4)]
        yp = [c.enter_context(nc.psum_tensor(f"{name}_yp{k}", [P, BT], F32)) for k in range(2)]

        pool_waited, dve_waited = sem("pool_waited"), sem("dve_waited")
        prefetched = sem("prefetched")
        hi_done, lo_done = sem("hi_done"), sem("lo_done")
        powers_set = sem("powers_set")
        stats_done = sem("stats_done")
        mv_done = sem("mv_done")
        work_done = sem("work_done")
        scale_done = sem("scale_done")
        xn_done = sem("xn_done")
        added = sem("added")
        tp_full = sem("tp_full")
        xt_read = sem("xt_read")
        xt_ready = sem("xt_ready")
        h_full = sem("h_full")
        h_read = sem("h_read")
        h_ready = sem("h_ready")
        dve_sq = sem("dve_sq")
        act_sq = sem("act_sq")
        pairs_added = sem("pairs_added")
        sq_added = sem("sq_added")
        ms_full = sem("ms_full")
        y_full = sem("y_full")
        y_done = sem("y_done")
        ms_done = sem("ms_done")
        rms_work = sem("rms_work")
        inv_done = sem("inv_done")
        in_loaded = [sem(f"in_loaded{k}") for k in range(2)]
        stored = [sem(f"stored{k}") for k in range(2)]
        bias_in = sem("bias_in")
        N = NB // 2
        Y_FULL0, Y_DONE0 = TB, 2
        block = c.enter_context(nc.Block())

        def tile(b, t):
            return TB * b + t

        @block.sync
        def _(sp):
            if jobs:
                sp.wait_ge(lo_done, len(jobs))
            prefetch(sp, loads, prefetched)
            if first_input is not None:
                def body(i):
                    for k in range(2):
                        b = 2 * i + k
                        if live(b, NB):
                            at_least(sp, added, b - 1)
                            sp.dma_start(x_in[:, k, :, :],
                                         first_input[bass.ds(b, 1), :, :].rearrange(
                                             "o (t p) d -> p (o t) d", p=P)
                                         ).then_inc(in_loaded[k], 16)
                body(0)
                with sp.Fori(1, N) as i:
                    body(i)
            if out_dram is not None:
                def body(i):
                    for k in range(2):
                        b = 2 * i + k
                        sp.wait_ge(y_done, Y_DONE0 + TB * (b + 1))
                        sp.dma_start(out_dram[bass.ds(b, 1), :, :].rearrange("o (t p) d -> p (o t) d", p=P),
                                     X[:, bass.ds(TB * b, TB), :]).then_inc(stored[k], 16)
                body(0)
                with sp.Fori(1, N) as i:
                    body(i)
                for k in range(2):
                    sp.wait_ge(stored[k], 16 * N)
            if loads:
                sp.wait_ge(prefetched, 16 * len(loads))

        @block.gpsimd
        def _(pool):
            for k, e in enumerate((-0.5, 0.5, -1.0)):
                nc.gpsimd.memset(powers[:, k, :], e).then_inc(powers_set, 1)
            if ternary:
                nc.gpsimd.memset(ones[:, :], 1.0).then_inc(powers_set, 1)
            pool.wait_ge(powers_set, 4 if ternary else 3)

            def scales(b, k):
                pool.wait_ge(mv_done, b + 1)
                at_least(pool, xn_done, b - 1)
                var = mv[:, k, :, 1]
                steps = 5 if ternary else 1
                if not ternary:
                    apart(pool, pool_waited)
                    nc.gpsimd.tensor_scalar(work[:, 0, :], var, EPS, None, ALU.add).then_inc(work_done, 1)
                    pool.wait_ge(work_done, steps * b + 1)
                    nc.gpsimd.tensor_tensor(scale[:, k, :], work[:, 0, :], powers[:, 0, :], ALU.pow
                                            ).then_inc(scale_done, 1)
                    return
                apart(pool, pool_waited)
                nc.gpsimd.tensor_scalar(work[:, 0, :], var, EPS, None, ALU.add).then_inc(work_done, 1)
                nc.gpsimd.tensor_tensor(work[:, 1, :], var, powers[:, 1, :], ALU.pow).then_inc(work_done, 1)
                pool.wait_ge(work_done, steps * b + 2)
                nc.gpsimd.tensor_tensor(work[:, 2, :], work[:, 0, :], powers[:, 1, :], ALU.pow
                                        ).then_inc(work_done, 1)
                pool.wait_ge(work_done, steps * b + 3)
                apart(pool, pool_waited)
                nc.gpsimd.tensor_scalar(work[:, 0, :], work[:, 2, :], 1e-8, None, ALU.mult).then_inc(work_done, 1)
                pool.wait_ge(work_done, steps * b + 4)
                nc.gpsimd.tensor_tensor(work[:, 2, :], work[:, 0, :], work[:, 1, :], ALU.add
                                        ).then_inc(work_done, 1)
                pool.wait_ge(work_done, steps * b + 5)
                nc.gpsimd.tensor_tensor(scale[:, k, :], work[:, 2, :], powers[:, 2, :], ALU.pow
                                        ).then_inc(scale_done, 1)

            def add_squares(b, k):
                pool.wait_ge(act_sq, MF // 2 * (b + 1))
                pool.wait_ge(dve_sq, MF // 2 * (b + 1))
                for m in range(1, MF, 2):
                    last = nc.gpsimd.tensor_tensor(h_sq[:, k, m, :], h_sq[:, k, m, :], h_sq[:, k, m - 1, :], ALU.add)
                last.then_inc(pairs_added, 1)
                pool.wait_ge(pairs_added, b + 1)
                for m in range(3, MF, 4):
                    last = nc.gpsimd.tensor_tensor(h_sq[:, k, m, :], h_sq[:, k, m, :], h_sq[:, k, m - 2, :], ALU.add)
                last.then_inc(sq_added, 1)

            def inverse_rms(b, k):
                pool.wait_ge(ms_done, b + 1)
                nc.gpsimd.tensor_tensor(rms[:, 0, :], ms[:, :], powers[:, 1, :], ALU.pow).then_inc(rms_work, 1)
                pool.wait_ge(rms_work, 2 * b + 1)
                apart(pool, pool_waited)
                nc.gpsimd.tensor_scalar(rms[:, 1, :], rms[:, 0, :], 1e-8, None, ALU.add).then_inc(rms_work, 1)
                pool.wait_ge(rms_work, 2 * b + 2)
                nc.gpsimd.tensor_tensor(inv_rms[:, k, :], rms[:, 1, :], powers[:, 2, :], ALU.pow
                                        ).then_inc(inv_done, 1)

            def body(i):
                for k in range(2):
                    b, q = 2 * i + k, 1 - k
                    if live(b, NB):
                        scales(b, k)
                    if ternary:
                        if live(b - 2, NB):
                            inverse_rms(b - 2, k)
                        if live(b - 1, NB):
                            add_squares(b - 1, q)
                    elif live(b, NB):
                        pool.wait_ge(xn_done, b + 1)
                        blk = X[:, bass.ds(TB * b, TB), :]
                        if first_input is not None:
                            pool.wait_ge(in_loaded[k], 16 * (i + 1))
                            apart(pool, pool_waited)
                            nc.gpsimd.tensor_tensor(blk, blk, x_in[:, k, :, :], ALU.add).then_inc(bias_in, 1)
                            pool.wait_ge(bias_in, b + 1)
                        apart(pool, pool_waited)
                        nc.gpsimd.tensor_tensor(blk, blk, out_bias[:, :].unsqueeze(1).to_broadcast([P, TB, D]),
                                                ALU.add).then_inc(added, 1)

            skewed(pool, body, N)

        @block.vector
        def _(dve):
            def statistics(b, k):
                at_least(dve, scale_done, b - 1)
                for t in range(TB):
                    nc.vector.bn_stats(stats[:, t, :], X[:, bass.ds(tile(b, t), 1), :].rearrange("p o d -> p (o d)")
                                       ).then_inc(stats_done, 1)
                dve.wait_ge(stats_done, TB * (b + 1))
                apart(dve, dve_waited)
                for t in range(TB):
                    last = nc.vector.bn_aggr(mv[:, k, t, :], stats[:, t, :])
                last.then_inc(mv_done, 1)

            def normalise(b, k):
                dve.wait_ge(scale_done, b + 1)
                at_least(dve, tp_full, KD * (b - 1))
                for t in range(TB):
                    last = nc.vector.tensor_scalar(xn[:, k, t, :],
                                                   X[:, bass.ds(tile(b, t), 1), :].rearrange("p o d -> p (o d)"),
                                                   mv[:, k, t, 0:1], scale[:, k, t:t + 1],
                                                   ALU.subtract, ALU.mult)
                last.then_inc(xn_done, 1)

            def hidden_low(b, k, ms_):
                for m in ms_:
                    dve.wait_ge(h_read, MF * b + m + 1)
                    if m == 0:
                        at_least(dve, y_full, Y_FULL0 + TB * (b - 1))
                    nc.vector.tensor_tensor(h_lo[:, k, m, :], h[:, m % 4, :], h_hi[:, k, m, :].bitcast(F32),
                                            ALU.subtract).then_inc(h_ready, 1)
                    if ternary and m % 2 == 0:
                        nc.vector.tensor_tensor(h_sq[:, k, m, :], h[:, m % 4, :], h[:, m % 4, :], ALU.mult
                                                ).then_inc(dve_sq, 1)

            def input_low(b, k):
                for j in range(KD):
                    dve.wait_ge(xt_read, KD * b + j + 1)
                    nc.vector.tensor_tensor(xt_lo[:, k, j, :], xt[:, j, :], xt_hi[:, k, j, :].bitcast(F32),
                                            ALU.subtract).then_inc(xt_ready, 1)

            def residual(b, k, t):
                n = TB * b + t
                row = X[:, bass.ds(tile(b, t), 1), :].rearrange("p o d -> p (o d)")
                if ternary:
                    if t == 0:
                        dve.wait_ge(inv_done, b + 1)
                    dve.wait_ge(y_full, Y_FULL0 + n + 1)
                    nc.vector.scalar_tensor_tensor(out=row, in0=yp[t % 2][:, 0:D], scalar=inv_rms[:, k, t:t + 1],
                                                   in1=row, op0=ALU.mult, op1=ALU.add).then_inc(y_done, 1)
                else:
                    dve.wait_ge(y_full, Y_FULL0 + n + 1)
                    if t == 0:
                        dve.wait_ge(added, b + 1)
                    nc.vector.tensor_tensor(row, yp[t % 2][:, 0:D], row, ALU.add).then_inc(y_done, 1)

            def mean_square(b):
                dve.wait_ge(ms_full, b + 1)
                nc.vector.tensor_scalar(ms[:, :], yp[1][:, D:D + TB], 1.0 / FF, None, ALU.mult
                                        ).then_inc(ms_done, 1)

            def body(i):
                for k in range(2):
                    b, q = 2 * i + k, 1 - k
                    if live(b, NB):
                        statistics(b, k)
                    if live(b - 1, NB):
                        hidden_low(b - 1, q, range(0, MF // 2))
                    if at_start(b):
                        low_halves(nc, dve, jobs, hi_done, lo_done)
                    if ternary and live(b - 2, NB):
                        mean_square(b - 2)
                    if live(b, NB):
                        normalise(b, k)
                    if live(b - 1, NB):
                        hidden_low(b - 1, q, range(MF // 2, MF))
                    if live(b - 2, NB):
                        residual(b - 2, k, 0)
                    if live(b, NB):
                        input_low(b, k)
                    if live(b - 2, NB):
                        for t in range(1, TB):
                            residual(b - 2, k, t)

            dve.sem_inc(y_done, Y_DONE0)
            skewed(dve, body, N)

        @block.scalar
        def _(act):
            def square(b, k, m):
                act.wait_ge(h_read, MF * b + m + 1)
                if m == 1:
                    at_least(act, ms_full, b - 1)
                nc.scalar.activation(h_sq[:, k, m, :], h[:, m % 4, :], ACT.Square).then_inc(act_sq, 1)

            def hidden(b, k):
                for m in range(MF):
                    act.wait_ge(h_full, MF * b + m + 1)
                    at_least(act, h_ready, MF * b + m - 3)
                    if ternary:
                        at_least(act, act_sq if m % 2 else dve_sq, MF // 2 * b + m // 2 - 1)
                    if m == 0:
                        at_least(act, y_full, Y_FULL0 + TB * (b - 1))
                    fn = ACT.Gelu if ternary else ACT.Silu
                    bias = 0.0 if ternary else hidden_bias[:, m:m + 1]
                    nc.scalar.activation(h[:, m % 4, :], hp[m % 4][:, :], fn, bias=bias)
                    nc.scalar.activation(h_hi[:, k, m, :], hp[m % 4][:, :], fn, bias=bias).then_inc(h_read, 1)
                    if ternary and m and m % 2 == 0:
                        square(b, k, m - 1)
                if ternary:
                    square(b, k, MF - 1)

            def inputs(b, k):
                for j in range(KD):
                    act.wait_ge(tp_full, KD * b + j + 1)
                    at_least(act, xt_ready, KD * (b - 1) + j + 1)
                    if j == 0:
                        at_least(act, h_full, MF * (b - 1))
                    for out in (xt[:, j, :], xt_hi[:, k, j, :]):
                        if ternary:
                            last = nc.scalar.activation(out, tp[j][:, :], ACT.Copy)
                        else:
                            last = nc.scalar.activation(out, tp[j][:, :], ACT.Identity,
                                                        bias=norm[:, 1, j:j + 1], scale=norm[:, 0, j:j + 1])
                    last.then_inc(xt_read, 1)

            def body(i):
                for k in range(2):
                    b, q = 2 * i + k, 1 - k
                    if live(b - 1, NB):
                        hidden(b - 1, q)
                    if live(b, NB):
                        inputs(b, k)

            high_halves(nc, jobs, hi_done)
            skewed(act, body, N)

        @block.tensor
        def _(pe):
            up_passes = [(xt_hi, w) for w in up] + [(xt_lo, up[0])]
            down_passes = [(h_hi, w) for w in down] + [(h_lo, down[0])]

            def up_product(b, k, between=None):
                for m in range(MF):
                    if m == MF // 2 + 1 and between is not None:
                        between()
                    if at_start(b) and m == 0 and jobs:
                        pe.wait_ge(lo_done, len(jobs))
                    if m == 0:
                        pe.wait_ge(xt_ready, KD * (b + 1))
                    at_least(pe, h_read, MF * b + m - 3)
                    todo = [(j, x, w) for j in range(KD) for x, w in up_passes]
                    for n, (j, x, w) in enumerate(todo):
                        last = nc.tensor.matmul(hp[m % 4][:, :], w[:, j, m * P:(m + 1) * P], x[:, k, j, :],
                                                start=(n == 0), stop=(n == len(todo) - 1))
                    last.then_inc(h_full, 1)

            def transposes(b, k):
                pe.wait_ge(xn_done, b + 1)
                for j in range(KD):
                    at_least(pe, xt_read, KD * (b - 1) + j + 1)
                    for t in range(TB):
                        last = nc.tensor.transpose(tp[j][:, t * P:(t + 1) * P], xn[:, k, t, j * P:(j + 1) * P],
                                                   ident[:, :])
                    last.then_inc(tp_full, 1)

            def square_sums(b, k):
                pe.wait_ge(sq_added, b + 1)
                pe.wait_ge(y_done, Y_DONE0 + TB * b)
                for t in range(TB):
                    for m in range(3, MF, 4):
                        last = nc.tensor.matmul(yp[1][:, D + t:D + t + 1], h_sq[:, k, m, t * P:(t + 1) * P],
                                                ones[:, :], start=(m == 3), stop=(m == MF - 1))
                last.then_inc(ms_full, 1)

            def down_product(b, k):
                pe.wait_ge(h_ready, MF * (b + 1))
                for t in range(TB):
                    if ternary and t == 1:
                        pe.wait_ge(ms_done, b + 1)
                    pe.wait_ge(y_done, Y_DONE0 + TB * b + t - 1)
                    todo = [(m, x, w) for m in range(MF) for x, w in down_passes]
                    for n, (m, x, w) in enumerate(todo):
                        last = nc.tensor.matmul(yp[t % 2][:, 0:D], x[:, k, m, t * P:(t + 1) * P], w[:, m, :],
                                                start=(n == 0), stop=(n == len(todo) - 1))
                    last.then_inc(y_full, 1)

            if ternary:
                pe.wait_ge(powers_set, 4)

            def body(i):
                for k in range(2):
                    b, q = 2 * i + k, 1 - k
                    sums = ternary and live(b - 2, NB)
                    if live(b - 1, NB):
                        up_product(b - 1, q, (lambda: square_sums(b - 2, k)) if sums else None)
                    elif sums:
                        square_sums(b - 2, k)
                    if live(b, NB):
                        transposes(b, k)
                    if live(b - 2, NB):
                        down_product(b - 2, k)

            pe.sem_inc(y_full, Y_FULL0)
            skewed(pe, body, N)

H, HD = 8, 32
HG = 4
NG = H // HG
CPB = S // BT


def retention_tables():
    half = HD // 2
    vec = (np.arange(0, HD, 2) + 0.4 * HD) / (1.4 * HD)
    pos = np.arange(S, dtype=np.float64)[:, None]
    power = (np.arange(S) % P / 128.0)[:, None]
    angle = pos * (1.0 / 10000.0 ** (np.arange(half, dtype=np.float64) / half))[None, :]
    up = vec[None, :] ** power

    def dup(m):
        return np.repeat(m, 2, axis=-1)

    cos = np.stack([dup(np.cos(angle) * up), dup(np.cos(angle) / up)], 1)
    sin = np.stack([dup(np.sin(angle) * up), dup(np.sin(angle) / up)], 1)
    sin[..., 0::2] *= -1.0
    rotary = np.stack([cos, sin], 1).reshape(S // P, P, 2, 2, HD).transpose(1, 0, 2, 3, 4)
    gamma = 1.0 - np.exp(np.linspace(np.log(1.0 / 32), np.log(1.0 / 128), H))
    p = np.arange(P, dtype=np.float64)[:, None]
    g = np.repeat(gamma, HD)[None, :]
    decay = np.stack([g ** -p, g ** p], 1)
    row = np.arange(P)
    state = np.zeros((P, NG, P))
    for j in range(NG):
        a = dup(vec)[row % HD] * gamma[HG * j + row // HD] ** P
        state[:, j, :] = a[:, None] * (row[:, None] // HD == row[None, :] // HD)
    causal = (row[None, :] >= row[:, None]).astype(np.float64)
    heads = (row[:, None] // HD == np.arange(HG)[None, :]).astype(np.float64)
    return {k: np.ascontiguousarray(v, np.float32) for k, v in
            dict(rotary=rotary, decay=decay, state_decay=state, causal=causal, heads=heads).items()}


def retention(nc, name, X, ident, *, qkv, gate, out_w, norm, gn, rotary, decay, state_decay, causal, heads, loads=(), jobs=()):
    with ExitStack() as c:
        def sb(n, shape, dt=F32):
            return c.enter_context(nc.sbuf_tensor(f"{name}_{n}", shape, dt))

        def sem(n):
            return nc.alloc_semaphore(f"{name}_{n}")

        stats = sb("stats", [P, TB, 6])
        mv = sb("mean_var", [P, 2, TB, 2])
        work = sb("scale_work", [P, TB])
        scale = sb("scale", [P, 2, TB])
        minus_half = sb("minus_half", [P, TB * H])
        xn = sb("xn", [P, TB, D])
        xt = sb("xt", [P, KD, BT])
        xt_hi = sb("xt_hi", [P, KD, BT], F32R)
        xt_lo = sb("xt_lo", [P, KD, BT], F32R)
        qk = sb("qk", [P, 4, 2, H, HD])
        qk_sin = sb("qk_sin", [P, 2, 2, H, HD])
        v = sb("v", [P, 4, D])
        qkt = sb("qkt", [P, 4, 2, NG, P])
        q_wide = sb("q_wide", [P, 2, NG, HG, P])
        pr = sb("probs", [P, 2, NG, HG, P])
        state = sb("state", [P, B, NG, P])
        state_in = sb("state_in", [P, NG, P])
        gt = sb("gate", [P, 2, KD, BT])
        y = sb("y", [P, 2, TB, D])
        y_sq = sb("y_sq", [P, TB, D])
        sums = sb("sums", [P, 2, TB * H])
        means = sb("means", [P, 3, TB * H])
        yt = sb("yt", [P, KD, BT])
        gy_hi = sb("gy_hi", [P, KD, BT], F32R)
        gy_lo = sb("gy_lo", [P, KD, BT], F32R)
        tr = [c.enter_context(nc.psum_tensor(f"{name}_tr{k}", [P, BT], F32)) for k in range(2)]
        pj = [c.enter_context(nc.psum_tensor(f"{name}_pj{k}", [P, BT], F32)) for k in range(2)]
        sc = [c.enter_context(nc.psum_tensor(f"{name}_sc{k}", [P, BT], F32)) for k in range(NG)]
        yp = c.enter_context(nc.psum_tensor(f"{name}_yp", [P, BT], F32))
        kv = c.enter_context(nc.psum_tensor(f"{name}_kv", [P, BT], F32))

        prefetched = sem("prefetched")
        hi_done, lo_done = sem("hi_done"), sem("lo_done")
        pool_waited, dve_waited = sem("pool_waited"), sem("dve_waited")
        consts_set = sem("consts_set")
        stats_done = sem("stats_done")
        mv_done = sem("mv_done")
        eps_added = sem("eps_added")
        scale_done = sem("scale_done")
        xn_done = sem("xn_done")
        tp_full = sem("tp_full")
        xt_read = sem("xt_read")
        xt_ready = sem("xt_ready")
        qk_full = sem("qk_full")
        qk_read = sem("qk_read")
        qk_done = sem("qk_done")
        v_full = sem("v_full")
        v_done = sem("v_done")
        g_full = sem("g_full")
        g_done = sem("g_done")
        tq_full = sem("tq_full")
        tq_done = sem("tq_done")
        sc_full = sem("sc_full")
        pr_done = sem("pr_done")
        kv_full = sem("kv_full")
        in_done = sem("in_done")
        y_full = sem("y_full")
        y_done = sem("y_done")
        state_done = sem("state_done")
        sum_done = sem("sum_done")
        mean_done = sem("mean_done")
        centred = sem("centred")
        sq_done = sem("sq_done")
        sq_sum_done = sem("sq_sum_done")
        var_done = sem("var_done")
        rstd_done = sem("rstd_done")
        yn_done = sem("yn_done")
        yt_full = sem("yt_full")
        yt_read = sem("yt_read")
        gy_done = sem("gy_done")
        gy_hi_done = sem("gy_hi_done")
        gy_ready = sem("gy_ready")
        wo_full = sem("wo_full")
        wo_done = sem("wo_done")
        N = NB // 2
        WO_DONE0, GY0, WO_FULL0 = 2, 1, 1
        block = c.enter_context(nc.Block())

        def place(i, k, lag):
            at, par = k - lag, (k - lag) % 2
            pair = i + at // 2
            return 2 * i + at, par, CPB * par + pair

        def xrow(blk, t, n=1):
            return X[:, bass.ds(TB * blk + t, n), :]

        @block.sync
        def _(sp):
            sp.wait_ge(lo_done, len(jobs))
            prefetch(sp, loads, prefetched)
            sp.wait_ge(prefetched, 16 * len(loads))

        @block.gpsimd
        def _(pool):
            nc.gpsimd.memset(minus_half[:, :], -0.5).then_inc(consts_set, 1)
            nc.gpsimd.memset(state[:, :, :, :], 0.0).then_inc(consts_set, 1)
            pool.wait_ge(consts_set, 2)

            def scales(b, k):
                pool.wait_ge(mv_done, b + 1)
                at_least(pool, xn_done, b - 1)
                apart(pool, pool_waited)
                nc.gpsimd.tensor_scalar(work[:, :], mv[:, k, :, 1], EPS, None, ALU.add).then_inc(eps_added, 1)
                pool.wait_ge(eps_added, b + 1)
                nc.gpsimd.tensor_tensor(scale[:, k, :], work[:, :], minus_half[:, 0:TB], ALU.pow
                                        ).then_inc(scale_done, 1)

            def rotary_sum(b, t):
                n = TB * b + t
                pool.wait_ge(qk_read, n + 1)
                nc.gpsimd.tensor_tensor(qk[:, t, :, :, :], qk[:, t, :, :, :], qk_sin[:, t % 2, :, :, :], ALU.add
                                        ).then_inc(qk_done, 1)

            def centre(b, k):
                pool.wait_ge(sum_done, b + 1)
                apart(pool, pool_waited)
                nc.gpsimd.tensor_scalar(means[:, 0, :], sums[:, 0, :], 1.0 / HD, None, ALU.mult
                                        ).then_inc(mean_done, 1)
                pool.wait_ge(mean_done, b + 1)
                groups = y[:, k, :, :].rearrange("p t (h d) -> p (t h) d", h=H)
                nc.gpsimd.tensor_tensor(groups, groups,
                                        means[:, 0, :].unsqueeze(2).to_broadcast([P, TB * H, HD]),
                                        ALU.subtract).then_inc(centred, 1)

            def group_rstd(b):
                pool.wait_ge(sq_sum_done, b + 1)
                apart(pool, pool_waited)
                nc.gpsimd.tensor_scalar(means[:, 1, :], sums[:, 1, :], 1.0 / HD, EPS, ALU.mult, ALU.add
                                        ).then_inc(var_done, 1)
                pool.wait_ge(var_done, b + 1)
                at_least(pool, yn_done, b)
                nc.gpsimd.tensor_tensor(means[:, 2, :], means[:, 1, :], minus_half[:, :], ALU.pow
                                        ).then_inc(rstd_done, 1)

            def gated(b, k):
                for j in range(KD):
                    pool.wait_ge(yt_read, KD * b + j + 1)
                    nc.gpsimd.tensor_tensor(yt[:, j, :], yt[:, j, :], gt[:, k, j, :], ALU.mult
                                            ).then_inc(gy_done, 1)

            def body(i):
                for k in range(2):
                    (s, k0, _), (s1, k1, _), (s2, k2, _) = (place(i, k, lag) for lag in range(3))
                    if live(s, NB):
                        scales(s, k0)
                    if live(s2, NB):
                        gated(s2, k2)
                    for t in range(TB):
                        if live(s, NB):
                            rotary_sum(s, t)
                        if t == 0 and live(s1, NB):
                            centre(s1, k1)
                        if t == 1 and live(s1, NB):
                            group_rstd(s1)

            skewed(pool, body, N)

        @block.vector
        def _(dve):
            dve.wait_ge(consts_set, 2)

            def statistics(b, k, blk):
                at_least(dve, scale_done, b - 1)
                for t in range(TB):
                    nc.vector.bn_stats(stats[:, t, :], xrow(blk, t).rearrange("p o d -> p (o d)")
                                       ).then_inc(stats_done, 1)
                dve.wait_ge(stats_done, TB * (b + 1))
                apart(dve, dve_waited)
                for t in range(TB):
                    last = nc.vector.bn_aggr(mv[:, k, t, :], stats[:, t, :])
                last.then_inc(mv_done, 1)

            def normalise(b, k, blk):
                dve.wait_ge(scale_done, b + 1)
                at_least(dve, tp_full, KD * b)
                for t in range(TB):
                    last = nc.vector.tensor_scalar(xn[:, t, :], xrow(blk, t).rearrange("p o d -> p (o d)"),
                                                   mv[:, k, t, 0:1], scale[:, k, t:t + 1],
                                                   ALU.subtract, ALU.mult)
                last.then_inc(xn_done, 1)

            def input_low(b):
                for j in range(KD):
                    dve.wait_ge(xt_read, KD * b + j + 1)
                    nc.vector.tensor_tensor(xt_lo[:, j, :], xt[:, j, :], xt_hi[:, j, :].bitcast(F32),
                                            ALU.subtract).then_inc(xt_ready, 1)

            def rotate(b, t, pair, bank):
                n = TB * b + t
                dve.wait_ge(qk_full, n + 1)
                at_least(dve, kv_full, n - 3)
                at_least(dve, qk_done, n - 1)
                src = pj[bank][:, :].rearrange("p (a h d) -> p a h d", a=2, h=H)
                tab = rotary[:, bass.ds(TB * pair + t, 1), :, :, :].rearrange("p o f a d -> p (o f) a d")
                cos = tab[:, 0, :, :].unsqueeze(2).to_broadcast([P, 2, H, HD])
                nc.vector.tensor_tensor(qk[:, t, :, :, :], src, cos, ALU.mult)
                for o in range(2):
                    sin = tab[:, 1, :, o::2].unsqueeze(2).to_broadcast([P, 2, H, HD // 2])
                    last = nc.vector.tensor_tensor(qk_sin[:, t % 2, :, :, o::2], src[:, :, :, 1 - o::2], sin,
                                                   ALU.mult)
                last.then_inc(qk_read, 1)

            def values(b, t, bank):
                n = TB * b + t
                dve.wait_ge(v_full, n + 1)
                at_least(dve, y_full, n - 3)
                nc.vector.tensor_tensor(v[:, t, :], pj[bank][:, 0:D], decay[:, 0, :], ALU.mult).then_inc(v_done, 1)

            def masked(b, t):
                n = TB * b + t
                for j in range(NG):
                    dve.wait_ge(sc_full, NG * n + j + 1)
                    if j == 0:
                        at_least(dve, y_full, n - 1)
                    nc.vector.tensor_tensor(pr[:, t % 2, j, :, :],
                                            sc[j][:, :].rearrange("p (h n) -> p h n", h=HG),
                                            causal[:, :].unsqueeze(1).to_broadcast([P, HG, P]),
                                            ALU.mult).then_inc(pr_done, 1)

            def outputs(b, t, k):
                n = TB * b + t
                dve.wait_ge(kv_full, n + 1)
                at_least(dve, state_done, n if t else n - TB)
                nc.vector.tensor_tensor(state_in[:, :, :], kv[:, 0:D].rearrange("p (j e) -> p j e", j=NG),
                                        state[:, k, :, :], ALU.add).then_inc(in_done, 1)
                dve.wait_ge(y_full, n + 1)
                if t == 0:
                    at_least(dve, yt_full, KD * (b - 1))
                nc.vector.tensor_tensor(y[:, k, t, :], yp[:, 0:D], decay[:, 1, :], ALU.mult).then_inc(y_done, 1)
                dve.wait_ge(in_done, n + 1)
                nc.vector.tensor_tensor(state[:, k, :, :], state_in[:, :, :], state_decay[:, :, :], ALU.mult
                                        ).then_inc(state_done, 1)

            def head_sums(b, k):
                dve.wait_ge(y_done, TB * (b + 1))
                at_least(dve, mean_done, b)
                nc.vector.tensor_reduce(sums[:, 0, :], y[:, k, :, :].rearrange("p t (h d) -> p (t h) d", h=H),
                                        axis=AX.X, op=ALU.add).then_inc(sum_done, 1)

            def square_sums(b):
                dve.wait_ge(sq_done, b + 1)
                at_least(dve, var_done, b)
                nc.vector.tensor_reduce(sums[:, 1, :], y_sq[:, :, :].rearrange("p t (h d) -> p (t h) d", h=H),
                                        axis=AX.X, op=ALU.add).then_inc(sq_sum_done, 1)

            def group_normalise(b, k):
                dve.wait_ge(rstd_done, b + 1)
                groups = y[:, k, :, :].rearrange("p t (h d) -> p (t h) d", h=H)
                nc.vector.tensor_tensor(groups, groups,
                                        means[:, 2, :].unsqueeze(2).to_broadcast([P, TB * H, HD]),
                                        ALU.mult).then_inc(yn_done, 1)

            def gated_low(b):
                for j in range(KD):
                    dve.wait_ge(gy_hi_done, KD * b + j + 1)
                    nc.vector.tensor_tensor(gy_lo[:, j, :], yt[:, j, :], gy_hi[:, j, :].bitcast(F32),
                                            ALU.subtract).then_inc(gy_ready, 1)

            def residual(b, half, blk):
                dve.wait_ge(wo_full, WO_FULL0 + 2 * b + half + 1)
                rows = xrow(blk, 2 * half, 2)
                nc.vector.tensor_tensor(rows, pj[1][:, :].rearrange("p (t d) -> p t d", t=2), rows, ALU.add
                                        ).then_inc(wo_done, 1)

            def body(i):
                for k in range(2):
                    (s, k0, blk), (s1, k1, _), (s2, k2, blk2) = (place(i, k, lag) for lag in range(3))
                    now, one, two = live(s, NB), live(s1, NB), live(s2, NB)
                    if now:
                        statistics(s, k0, blk)
                    if one:
                        masked(s1, 2)
                    if now:
                        normalise(s, k0, blk)
                    if one:
                        outputs(s1, 1, k1)
                    if at_start(s):
                        low_halves(nc, dve, jobs, hi_done, lo_done)
                    if one:
                        masked(s1, 3)
                        outputs(s1, 2, k1)
                    if now:
                        input_low(s)
                    if one:
                        outputs(s1, 3, k1)
                    if now:
                        rotate(s, 0, i, 0)
                        values(s, 0, 1)
                    if one:
                        head_sums(s1, k1)
                    if two:
                        gated_low(s2)
                    if now:
                        rotate(s, 1, i, 1)
                        values(s, 1, 0)
                    if one:
                        square_sums(s1)
                    if two:
                        residual(s2, 0, blk2)
                    if now:
                        rotate(s, 2, i, 0)
                        values(s, 2, 1)
                        masked(s, 0)
                    if one:
                        group_normalise(s1, k1)
                    if now:
                        rotate(s, 3, i, 1)
                        values(s, 3, 0)
                        masked(s, 1)
                        outputs(s, 0, k0)
                    if two:
                        residual(s2, 1, blk2)

            dve.sem_inc(wo_done, WO_DONE0)
            dve.sem_inc(gy_ready, GY0)
            skewed(dve, body, N)

        @block.scalar
        def _(act):
            def inputs(b):
                for j in range(KD):
                    act.wait_ge(tp_full, KD * b + j + 1)
                    if j == 0:
                        at_least(act, v_full, TB * b)
                        at_least(act, xt_ready, KD * b)
                    bank = tr[1 - j]
                    nc.scalar.activation(xt[:, j, :], bank[:, :], ACT.Identity,
                                         bias=norm[:, 1, j:j + 1], scale=norm[:, 0, j:j + 1])
                    nc.scalar.activation(xt_hi[:, j, :], bank[:, :], ACT.Identity,
                                         bias=norm[:, 1, j:j + 1], scale=norm[:, 0, j:j + 1]
                                         ).then_inc(xt_read, 1)

            def heads_out(b, t, bank):
                n = TB * b + t
                act.wait_ge(tq_full, n + 1)
                at_least(act, y_full, n - 3)
                at_least(act, sc_full, NG * (n - 1))
                nc.scalar.activation(qkt[:, t, :, :, :].rearrange("p a j n -> p (a j n)"), tr[bank][:, :], ACT.Copy)
                for j in range(NG):
                    for h in range(HG):
                        last = nc.scalar.activation(q_wide[:, t % 2, j, h, :], tr[bank][:, j * P:(j + 1) * P],
                                                    ACT.Copy, scale=heads[:, h:h + 1])
                last.then_inc(tq_done, 1)

            def gates(b, k, j):
                act.wait_ge(g_full, KD * b + j + 1)
                at_least(act, gy_done, KD * (b - 1))
                nc.scalar.activation(gt[:, k, j, :], pj[0][:, :], ACT.Silu).then_inc(g_done, 1)

            def squares(b, k):
                act.wait_ge(centred, b + 1)
                at_least(act, sq_sum_done, b)
                nc.scalar.activation(y_sq[:, :, :], y[:, k, :, :], ACT.Square).then_inc(sq_done, 1)

            def normed(b):
                for j in range(KD):
                    act.wait_ge(yt_full, KD * b + j + 1)
                    at_least(act, gy_ready, GY0 + KD * b)
                    nc.scalar.activation(yt[:, j, :], tr[1 - j][:, :], ACT.Identity,
                                         bias=gn[:, 1, j:j + 1], scale=gn[:, 0, j:j + 1]).then_inc(yt_read, 1)

            def gated_high(b):
                for j in range(KD):
                    act.wait_ge(gy_done, KD * b + j + 1)
                    if j == 0:
                        at_least(act, wo_full, WO_FULL0 + 2 * b)
                    nc.scalar.activation(gy_hi[:, j, :], yt[:, j, :], ACT.Copy).then_inc(gy_hi_done, 1)

            def body(i):
                for k in range(2):
                    (s, k0, _), (s1, k1, _), (s2, k2, _) = (place(i, k, lag) for lag in range(3))
                    now, one, two = live(s, NB), live(s1, NB), live(s2, NB)
                    if one:
                        heads_out(s1, 3, 0)
                    if now:
                        inputs(s)
                    if two:
                        normed(s2)
                        gated_high(s2)
                    if now:
                        gates(s, k0, 0)
                    if one:
                        squares(s1, k1)
                    if now:
                        heads_out(s, 0, 1)
                        heads_out(s, 1, 0)
                        gates(s, k0, 1)
                        heads_out(s, 2, 1)

            high_halves(nc, jobs, hi_done)
            skewed(act, body, N)

        @block.tensor
        def _(pe):
            def transposes(b):
                pe.wait_ge(xn_done, b + 1)
                for j in range(KD):
                    at_least(pe, tq_done, TB * b - 1 + j)
                    for t in range(TB):
                        last = nc.tensor.transpose(tr[1 - j][:, t * P:(t + 1) * P], xn[:, t, j * P:(j + 1) * P],
                                                   ident[:, :])
                    last.then_inc(tp_full, 1)

            def three(out, x, w):
                todo = [(j, a, c_) for j in range(KD) for a, c_ in ((0, 0), (0, 1), (1, 0))]
                for n, (j, a, c_) in enumerate(todo):
                    last = nc.tensor.matmul(out, x(a, j), w(c_, j), start=(n == 0), stop=(n == len(todo) - 1))
                return last

            xs = (xt_hi, xt_lo)

            def project(b, t, bank):
                n = TB * b + t
                if at_start(b) and t == 0:
                    pe.wait_ge(lo_done, len(jobs))
                if t == 0:
                    pe.wait_ge(xt_ready, KD * (b + 1))
                    at_least(pe, v_done, n)
                if t == 1:
                    pe.wait_ge(v_done, n)
                if t == 2:
                    pe.wait_ge(v_done, n)
                if t == 3:
                    pe.wait_ge(v_done, n)
                three(pj[bank][:, :], lambda a, j: xs[a][:, j, t * P:(t + 1) * P],
                      lambda a, j: qkv[a][:, j, 0:2 * D]).then_inc(qk_full, 1)
                if t == 0:
                    at_least(pe, qk_read, n)
                    at_least(pe, wo_done, WO_DONE0 + 2 * (b - 2))
                if t == 1:
                    pe.wait_ge(g_done, KD * b + 1)
                if t == 2:
                    pe.wait_ge(qk_read, n)
                    at_least(pe, wo_done, WO_DONE0 + 2 * (b - 2) + 1)
                if t == 3:
                    pe.wait_ge(g_done, KD * b + 2)
                three(pj[1 - bank][:, 0:D], lambda a, j: xs[a][:, j, t * P:(t + 1) * P],
                      lambda a, j: qkv[a][:, j, 2 * D:3 * D]).then_inc(v_full, 1)

            def gate_product(b, m):
                pe.wait_ge(qk_read, TB * b + 2 * m + 1)
                three(pj[0][:, :], lambda a, j: gate[a][:, j, m * P:(m + 1) * P],
                      lambda a, j: xs[a][:, j, :]).then_inc(g_full, 1)

            def transpose_heads(b, t, bank):
                n = TB * b + t
                pe.wait_ge(qk_done, n + 1)
                if t == 0 or t == 1:
                    at_least(pe, yt_read, KD * (b - 2) + t + 1)
                else:
                    at_least(pe, tq_done, n - 1)
                for f in range(2):
                    for j in range(NG):
                        col = (f * NG + j) * P
                        last = nc.tensor.transpose(
                            tr[bank][:, col:col + P],
                            qk[:, t, f, HG * j:HG * (j + 1), :].rearrange("p h d -> p (h d)"), ident[:, :])
                last.then_inc(tq_full, 1)

            def scores(b, t):
                n = TB * b + t
                pe.wait_ge(tq_done, n + 1)
                for j in range(NG):
                    at_least(pe, pr_done, NG * n + j - 1)
                    nc.tensor.matmul(sc[j][:, :], qkt[:, t, 1, j, :],
                                     q_wide[:, t % 2, j, :, :].rearrange("p h n -> p (h n)"),
                                     start=True, stop=True).then_inc(sc_full, 1)

            def chunk_out(b, t, k):
                n = TB * b + t
                pe.wait_ge(v_done, n + 1)
                at_least(pe, in_done, n)
                for j in range(NG):
                    last = nc.tensor.matmul(kv[:, j * P:(j + 1) * P],
                                            qk[:, t, 1, HG * j:HG * (j + 1), :].rearrange("p h d -> p (h d)"),
                                            v[:, t, j * P:(j + 1) * P], start=True, stop=True)
                last.then_inc(kv_full, 1)
                at_least(pe, y_done, n)
                if t:
                    pe.wait_ge(state_done, n)
                else:
                    at_least(pe, state_done, n - TB)
                for j in range(NG):
                    nc.tensor.matmul(yp[:, j * P:(j + 1) * P], qkt[:, t, 0, j, :], state[:, k, j, :],
                                     start=True, stop=False)
                    pe.wait_ge(pr_done, NG * n + j + 1)
                    for h in range(HG):
                        e = (HG * j + h) * HD
                        last = nc.tensor.matmul(yp[:, e:e + HD], pr[:, t % 2, j, h, :], v[:, t, e:e + HD],
                                                start=False, stop=(h == HG - 1))
                last.then_inc(y_full, 1)

            def transpose_outputs(b, k, s):
                pe.wait_ge(yn_done, b + 1)
                for j in range(KD):
                    if live(s, NB):
                        pe.wait_ge(xt_read, KD * s + j + 1)
                    elif isinstance(s, int) and s == NB:
                        pe.wait_ge(tq_done, TB * s - 1 + j)
                    else:
                        pe.wait_ge(yt_read, KD * b - 1 + j)
                    for t in range(TB):
                        last = nc.tensor.transpose(tr[1 - j][:, t * P:(t + 1) * P],
                                                   y[:, k, t, j * P:(j + 1) * P], ident[:, :])
                    last.then_inc(yt_full, 1)

            def out_product(b, half):
                if half == 0:
                    pe.wait_ge(gy_ready, GY0 + KD * (b + 1))
                gys = (gy_hi, gy_lo)
                for t in (2 * half, 2 * half + 1):
                    last = three(pj[1][:, (t % 2) * D:(t % 2 + 1) * D],
                                 lambda a, j: gys[a][:, j, t * P:(t + 1) * P],
                                 lambda a, j: out_w[a][:, j, :])
                last.then_inc(wo_full, 1)

            pe.wait_ge(consts_set, 2)
            pe.sem_inc(wo_full, WO_FULL0)

            def body(i):
                for k in range(2):
                    (s, k0, _), (s1, k1, _), (s2, k2, _) = (place(i, k, lag) for lag in range(3))
                    now, one, two = live(s, NB), live(s1, NB), live(s2, NB)
                    if one:
                        transpose_heads(s1, 3, 0)
                        scores(s1, 2)
                        chunk_out(s1, 1, k1)
                        scores(s1, 3)
                    if now:
                        transposes(s)
                    if one:
                        chunk_out(s1, 2, k1)
                    if two:
                        transpose_outputs(s2, k2, s)
                    if one:
                        chunk_out(s1, 3, k1)
                    if now:
                        project(s, 0, 0)
                        gate_product(s, 0)
                        project(s, 1, 1)
                        transpose_heads(s, 0, 1)
                    if two:
                        if now:
                            pe.wait_ge(qk_read, TB * s + 2)
                        else:
                            pe.wait_ge(qk_read, TB * NB)
                            pe.wait_ge(wo_done, WO_DONE0 + 2 * s2)
                        out_product(s2, 0)
                    if now:
                        project(s, 2, 0)
                        transpose_heads(s, 1, 0)
                        scores(s, 0)
                        gate_product(s, 1)
                        project(s, 3, 1)
                        transpose_heads(s, 2, 1)
                        scores(s, 1)
                    if two:
                        if now:
                            pe.wait_ge(qk_read, TB * s + 4)
                        else:
                            pe.wait_ge(wo_done, WO_DONE0 + 2 * s2 + 1)
                        out_product(s2, 1)
                    if now:
                        chunk_out(s, 0, k0)

            skewed(pe, body, N)

WH, WKV, WD = 16, 4, 16
WIN = 64
NC = P // WIN
PAIRS = WH // WKV // 2
SEG = 32
MASKED = -1e30


def window_tables():
    half = WD // 2
    inv = (1.0 / 10000.0 ** (np.arange(0, WD, 2, dtype=np.float32) / WD)).astype(np.float32)
    angle = np.arange(S, dtype=np.float32)[:, None] * inv[None, :]
    cos, sin = np.cos(angle), np.sin(angle)
    tab = np.stack([np.concatenate([cos, cos], 1), np.concatenate([sin, -sin], 1)], 1)
    tab = tab.reshape(S // P, P, 2, WD).transpose(1, 0, 2, 3)
    n = (np.arange(P) % WIN)[:, None]
    m = np.arange(WIN)[None, :]
    own, before = np.where(m <= n, 0.0, MASKED), np.where(m > n, 0.0, MASKED)
    none = np.full((P, WIN), MASKED)
    mask = np.zeros((P, 2, NC, PAIRS, P))
    for v, b in ((0, none), (1, before)):
        mask[:, v, 0] = np.concatenate([own, b], 1)[:, None, :]
        mask[:, v, 1] = np.concatenate([before, own], 1)[:, None, :]
    return {"win_rotary": np.ascontiguousarray(tab, np.float32), "win_masks": mask.astype(np.float32)}


def window_weights(nc, name, wo, mix, out_hi, out_lo, gain, jobs):
    with ExitStack() as c:
        mixed = c.enter_context(nc.sbuf_tensor(f"{name}_mixed", [P, 2, 2, D], F32))
        first, whole, high, hi_done = (nc.alloc_semaphore(f"{name}_{s}")
                                       for s in ("first", "whole", "high", "hi_done"))
        block = c.enter_context(nc.Block())

        @block.gpsimd
        def _(pool):
            nc.gpsimd.memset(gain[:, WH:WH + WKV], 1.0)
            nc.gpsimd.tensor_scalar(gain[:, 0:WH], gain[:, 0:WH], WD ** -0.5, None, ALU.mult)

        @block.scalar
        def _(act):
            high_halves(nc, jobs, hi_done)

        @block.vector
        def _(dve):
            for a in range(2):
                nc.vector.tensor_scalar(mixed[:, 0, a, :], wo[:, 0, :], mix[:, 0, a:a + 1], None, ALU.mult
                                        ).then_inc(first, 1)
            for a in range(2):
                dve.wait_ge(first, a + 1)
                nc.vector.scalar_tensor_tensor(out=mixed[:, 1, a, :], in0=wo[:, 1, :], scalar=mix[:, 1, a:a + 1],
                                               in1=mixed[:, 0, a, :], op0=ALU.mult, op1=ALU.add
                                               ).then_inc(whole, 1)
            for a in range(2):
                dve.wait_ge(whole, a + 1)
                nc.vector.tensor_copy(out_hi[:, a, :], mixed[:, 1, a, :]).then_inc(high, 1)
            for a in range(2):
                dve.wait_ge(high, a + 1)
                nc.vector.tensor_tensor(out_lo[:, a, :], mixed[:, 1, a, :], out_hi[:, a, :].bitcast(F32),
                                        ALU.subtract)
            low_halves(nc, dve, jobs, hi_done)


def window_attention(nc, name, X, ident, *, qkv, out_w, gain, win_rotary, win_masks):
    R = 4
    with ExitStack() as c:
        def sb(n, shape, dt=F32):
            return c.enter_context(nc.sbuf_tensor(f"{name}_{n}", shape, dt))

        def sem(n):
            return nc.alloc_semaphore(f"{name}_{n}")

        NH = WH + WKV
        QKV = (WH + 2 * WKV) * WD
        masks = sb("masks", [P, 2, NC * PAIRS * P], BF16)
        ident_b = sb("ident_b", [P, P], BF16)
        stats = sb("stats", [P, 2, 6])
        mv = sb("mean_var", [P, 2, 2])
        work = sb("work", [P, 1])
        scale = sb("scale", [P, 2, 1])
        minus_half = sb("minus_half", [P, NH])
        xn = sb("xn", [P, 2, D])
        xt_hi = sb("xt_hi", [P, 2, KD, P], F32R)
        xt_lo = sb("xt_lo", [P, 2, KD, P], F32R)
        raw = sb("raw", [P, 2, QKV])
        sq = sb("sq", [P, NH * WD])
        sq_sum = sb("sq_sum", [P, NH])
        rms = sb("rms", [P, 3, NH])
        rot = sb("rot", [P, 2, NH, WD])
        padded = sb("padded", [P, 2, NH // WKV, WKV, SEG])
        qt = sb("qt", [P, 2, PAIRS, NC, P])
        kt = sb("kt", [P, R, WKV, 4, WIN])
        v_odd = sb("v_odd", [P, R, WKV, WD + 1])
        v_even = sb("v_even", [P, R, WKV, WD + 1])
        minus_top = sb("minus_top", [P, WKV, NC * PAIRS])
        pr = sb("probs", [P, WKV, NC * PAIRS, P])
        pt = sb("probs_t", [P, WKV, NC * PAIRS, P])
        inv = sb("inv", [P, 2, NC * PAIRS * WKV])
        yn = sb("yn", [P, NC, PAIRS * WKV * WD])
        yt_hi = sb("yt_hi", [P, 2, NC, WIN], F32R)
        yt_lo = sb("yt_lo", [P, 2, NC, WIN], F32R)
        sc = [c.enter_context(nc.psum_tensor(f"{name}_sc{g}", [P, BT], F32)) for g in range(WKV)]
        wide = c.enter_context(nc.psum_tensor(f"{name}_wide", [P, BT], F32))
        yp = c.enter_context(nc.psum_tensor(f"{name}_yp", [P, BT], F32))
        pj = c.enter_context(nc.psum_tensor(f"{name}_pj", [P, BT], F32))
        tr = c.enter_context(nc.psum_tensor(f"{name}_tr", [P, BT], F32))

        pool_waited, dve_waited = sem("pool_waited"), sem("dve_waited")
        consts_set = sem("consts_set")
        masks_set = sem("masks_set")
        stats_done = sem("stats_done")
        mv_done = sem("mv_done")
        eps_added = sem("eps_added")
        scale_done = sem("scale_done")
        xn_done = sem("xn_done")
        tp_full = sem("tp_full")
        xt_hi_done = sem("xt_hi_done")
        xt_ready = sem("xt_ready")
        qkv_full = sem("qkv_full")
        raw_done = sem("raw_done")
        sq_done = sem("sq_done")
        sq_sum_done = sem("sq_sum_done")
        rms_work = sem("rms_work")
        rms_done = sem("rms_done")
        rot_done = sem("rot_done")
        rot_sum_done = sem("rot_sum_done")
        v_work = sem("v_work")
        v_done = sem("v_done")
        padded_done = sem("padded_done")
        tq_full = sem("tq_full")
        tk_full = sem("tk_full")
        qt_done = sem("qt_done")
        kt_done = sem("kt_done")
        kt_moved = sem("kt_moved")
        sc_full = sem("sc_full")
        top_done = sem("top_done")
        exp_done = sem("exp_done")
        pt_full = sem("pt_full")
        pt_done = sem("pt_done")
        y_full = sem("y_full")
        inv_done = sem("inv_done")
        yn_done = sem("yn_done")
        yt_full = sem("yt_full")
        yt_hi_done = sem("yt_hi_done")
        yt_ready = sem("yt_ready")
        wo_full = sem("wo_full")
        wo_done = sem("wo_done")
        U = R
        N = NT // U
        C0 = 1
        block = c.enter_context(nc.Block())

        def row(i, k, lag):
            at = k - lag
            return bass.ds((U // 2) * i + at // 2 + (NT // 2) * (at % 2), 1)

        @block.gpsimd
        def _(pool):
            nc.gpsimd.memset(minus_half[:, :], -0.5).then_inc(consts_set, 1)
            nc.gpsimd.memset(padded[:, :, :, :, :], 0.0).then_inc(consts_set, 1)
            nc.gpsimd.memset(kt[:, :, :, :, :], 0.0).then_inc(consts_set, 1)
            nc.gpsimd.memset(v_even[:, :, :, :], 0.0).then_inc(consts_set, 1)
            nc.gpsimd.memset(v_odd[:, :, :, WD], 1.0).then_inc(consts_set, 1)
            pool.wait_ge(consts_set, 5)
            nc.gpsimd.memset(v_even[:, :, :, WD], 1.0).then_inc(consts_set, 1)
            pool.wait_ge(consts_set, 6)

            def norm_scale(n, k):
                pool.wait_ge(mv_done, n + 1)
                at_least(pool, xn_done, n - 1)
                apart(pool, pool_waited)
                nc.gpsimd.tensor_scalar(work[:, :], mv[:, k % 2, 1:2], EPS, None, ALU.add).then_inc(eps_added, 1)
                pool.wait_ge(eps_added, n + 1)
                nc.gpsimd.tensor_tensor(scale[:, k % 2, :], work[:, :], minus_half[:, 0:1], ALU.pow
                                        ).then_inc(scale_done, 1)

            def squares(n, k):
                pool.wait_ge(raw_done, n + 1)
                at_least(pool, sq_sum_done, n)
                qk_cols = raw[:, k % 2, 0:NH * WD]
                nc.gpsimd.tensor_tensor(sq[:, :], qk_cols, qk_cols, ALU.mult).then_inc(sq_done, 1)

            def values(n, k):
                r = k % R
                at_least(pool, y_full, WKV * (n - 1))
                v_cols = raw[:, k % 2, NH * WD:QKV].rearrange("p (g d) -> p g d", g=WKV)
                apart(pool, pool_waited)
                nc.gpsimd.tensor_copy(v_odd[:, r, :, 0:WD], v_cols).then_inc(v_work, 1)
                pool.wait_ge(v_work, 2 * n + 1)
                apart(pool, pool_waited)
                nc.gpsimd.tensor_copy(v_even[0:WIN, r, :, 0:WD], v_cols[0:WIN]).then_inc(v_work, 1)
                pool.wait_ge(v_work, 2 * n + 2)
                apart(pool, pool_waited)
                nc.gpsimd.tensor_copy(v_even[WIN:P, (r + 2) % R, :, 0:WD], v_cols[WIN:P]).then_inc(v_done, 1)
                pool.wait_ge(v_done, n + 1)

            def head_scales(n):
                pool.wait_ge(sq_sum_done, n + 1)
                apart(pool, pool_waited)
                nc.gpsimd.tensor_scalar(rms[:, 0, :], sq_sum[:, :], 1.0 / WD, 1e-6, ALU.mult, ALU.add
                                        ).then_inc(rms_work, 1)
                pool.wait_ge(rms_work, 2 * n + 1)
                nc.gpsimd.tensor_tensor(rms[:, 1, :], rms[:, 0, :], minus_half[:, :], ALU.pow
                                        ).then_inc(rms_work, 1)
                pool.wait_ge(rms_work, 2 * n + 2)
                at_least(pool, padded_done, n)
                nc.gpsimd.tensor_tensor(rms[:, 2, :], rms[:, 1, :], gain[:, :], ALU.mult).then_inc(rms_done, 1)

            def even_keys(n, k):
                r = k % R
                pool.wait_ge(kt_done, n + 1)
                at_least(pool, sc_full, WKV * (n - 1))
                apart(pool, pool_waited)
                nc.gpsimd.tensor_copy(kt[:, r, :, 2, :], kt[:, r, :, 0, :])
                nc.gpsimd.tensor_copy(kt[:, (r + 2) % R, :, 3, :], kt[:, r, :, 1, :]).then_inc(kt_moved, 1)

            def body(i):
                for k in range(U):
                    n = U * i + k
                    if live(n - 2, NT):
                        even_keys(n - 2, k - 2)
                    if live(n - 1, NT):
                        squares(n - 1, k - 1)
                    if live(n, NT):
                        norm_scale(n, k)
                    if live(n - 1, NT):
                        head_scales(n - 1)
                        values(n - 1, k - 1)

            skewed(pool, body, N)

        @block.vector
        def _(dve):
            nc.vector.tensor_copy(masks[:, :, :], win_masks.rearrange("p v c u m -> p v (c u m)")
                                  ).then_inc(masks_set, 1)
            nc.vector.tensor_copy(ident_b[:, :], ident[:, :]).then_inc(masks_set, 1)
            dve.wait_ge(consts_set, 6)
            dve.sem_inc(yt_ready, C0)
            dve.sem_inc(wo_done, C0)

            def statistics(n, i, k):
                at_least(dve, scale_done, n - 1)
                nc.vector.bn_stats(stats[:, k % 2, :], X[:, row(i, k, 0), :].rearrange("p o d -> p (o d)")
                                   ).then_inc(stats_done, 1)
                dve.wait_ge(stats_done, n + 1)
                apart(dve, dve_waited)
                nc.vector.bn_aggr(mv[:, k % 2, :], stats[:, k % 2, :]).then_inc(mv_done, 1)

            def normalise(n, i, k):
                dve.wait_ge(scale_done, n + 1)
                at_least(dve, tp_full, n - 1)
                nc.vector.tensor_scalar(xn[:, k % 2, :], X[:, row(i, k, 0), :].rearrange("p o d -> p (o d)"),
                                        mv[:, k % 2, 0:1], scale[:, k % 2, :], ALU.subtract, ALU.mult
                                        ).then_inc(xn_done, 1)

            def input_low(n, k):
                dve.wait_ge(xt_hi_done, n + 1)
                nc.vector.tensor_tensor(xt_lo[:, k % 2, :, :], tr[:, 0:D].rearrange("p (j t) -> p j t", j=KD),
                                        xt_hi[:, k % 2, :, :].bitcast(F32), ALU.subtract).then_inc(xt_ready, 1)

            def rotate(n, i, k):
                dve.wait_ge(raw_done, n + 1)
                at_least(dve, padded_done, n)
                par = (k - 1) % 2
                src = raw[:, par, 0:NH * WD].rearrange("p (h d) -> p h d", h=NH)
                tab = win_rotary[:, bass.ds((U // 2) * i + (k - 1) // 2, 1), :, :].rearrange(
                    "p o f d -> p (o f) d")
                hd = WD // 2
                nc.vector.tensor_tensor(rot[:, 0, :, :], src,
                                        tab[:, 0, :].unsqueeze(1).to_broadcast([P, NH, WD]), ALU.mult)
                for o in range(2):
                    last = nc.vector.tensor_tensor(
                        rot[:, 1, :, o * hd:(o + 1) * hd], src[:, :, (1 - o) * hd:(2 - o) * hd],
                        tab[:, 1, o * hd:(o + 1) * hd].unsqueeze(1).to_broadcast([P, NH, hd]), ALU.mult)
                last.then_inc(rot_done, 1)

            def square_sums(n):
                dve.wait_ge(sq_done, n + 1)
                at_least(dve, rms_work, 2 * n)
                nc.vector.tensor_reduce(sq_sum[:, :], sq[:, :].rearrange("p (h d) -> p h d", h=NH),
                                        axis=AX.X, op=ALU.add).then_inc(sq_sum_done, 1)

            def rotary_sum(n):
                dve.wait_ge(rot_done, n + 1)
                nc.vector.tensor_tensor(rot[:, 0, :, :], rot[:, 0, :, :], rot[:, 1, :, :], ALU.add
                                        ).then_inc(rot_sum_done, 1)

            def pad(n, k):
                dve.wait_ge(rot_sum_done, n + 1)
                dve.wait_ge(rms_done, n + 1)
                at_least(dve, tk_full, n - 1)
                nc.vector.tensor_tensor(
                    padded[:, k % 2, :, :, 0:WD].rearrange("p c g d -> p (c g) d"), rot[:, 0, :, :],
                    rms[:, 2, :].unsqueeze(2).to_broadcast([P, NH, WD]), ALU.mult).then_inc(padded_done, 1)

            def row_max(n, g):
                dve.wait_ge(sc_full, WKV * n + g + 1)
                at_least(dve, exp_done, WKV * (n - 1) + g + 1)
                nc.vector.tensor_reduce(minus_top[:, g, :], sc[g][:, :].rearrange("p (c m) -> p c m", m=P),
                                        axis=AX.X, op=ALU.max, negate=True).then_inc(top_done, 1)

            def divide(n, k):
                dve.wait_ge(y_full, WKV * (n + 1))
                rows = yp[:, 0:NC * PAIRS * WKV * (WD + 1)].rearrange("p (c e) -> p c e", e=WD + 1)
                nc.vector.reciprocal(inv[:, k % 2, :], rows[:, :, WD]).then_inc(inv_done, 1)
                dve.wait_ge(inv_done, n + 1)
                at_least(dve, yt_full, C0 + n)
                nc.vector.tensor_tensor(yn[:, :, :].rearrange("p c (e d) -> p (c e) d", d=WD), rows[:, :, 0:WD],
                                        inv[:, k % 2, :].unsqueeze(2).to_broadcast([P, NC * PAIRS * WKV, WD]),
                                        ALU.mult).then_inc(yn_done, 1)

            def output_low(n):
                dve.wait_ge(yt_hi_done, n + 1)
                nc.vector.tensor_tensor(yt_lo[:, :, :, :].rearrange("p a c n -> p c a n"),
                                        tr[:, 0:D].rearrange("p (c a n) -> p c a n", c=NC, a=2),
                                        yt_hi[:, :, :, :].bitcast(F32).rearrange("p a c n -> p c a n"),
                                        ALU.subtract).then_inc(yt_ready, 1)

            def residual(n, i, k):
                dve.wait_ge(wo_full, C0 + n + 1)
                x_row = X[:, row(i, k, 4), :].rearrange("p o d -> p (o d)")
                nc.vector.tensor_tensor(x_row, pj[:, 0:D], x_row, ALU.add).then_inc(wo_done, 1)

            def body(i):
                for k in range(U):
                    n = U * i + k
                    if live(n - 4, NT):
                        divide(n - 4, k)
                    if live(n, NT):
                        statistics(n, i, k)
                    if live(n - 1, NT):
                        rotate(n - 1, i, k)
                        square_sums(n - 1)
                    if live(n - 2, NT):
                        row_max(n - 2, 0)
                    if live(n, NT):
                        normalise(n, i, k)
                    if live(n - 1, NT):
                        rotary_sum(n - 1)
                    if live(n - 2, NT):
                        row_max(n - 2, 1)
                    if live(n - 4, NT):
                        output_low(n - 4)
                    if live(n - 1, NT):
                        pad(n - 1, k - 1)
                    if live(n - 2, NT):
                        row_max(n - 2, 2)
                    if live(n, NT):
                        input_low(n, k)
                    if live(n - 2, NT):
                        row_max(n - 2, 3)
                    if live(n - 4, NT):
                        residual(n - 4, i, k)

            skewed(dve, body, N)

        @block.scalar
        def _(act):
            def queries_out(n, k):
                act.wait_ge(tq_full, n + 1)
                at_least(act, sc_full, WKV * (n - 1))
                nc.scalar.activation(qt[:, k % 2, :, :, :].rearrange("p u c n -> p (u c n)"), wide[:, :], ACT.Copy
                                     ).then_inc(qt_done, 1)

            def keys_out(n, k):
                act.wait_ge(tk_full, n + 1)
                at_least(act, sc_full, WKV * (n - 3))
                for g in range(WKV):
                    part = slice(SEG * g, SEG * (g + 1))
                    last = nc.scalar.activation(kt[part, k % R, g, 0:2, :].rearrange("p c n -> p (c n)"),
                                                tr[part, 0:P], ACT.Copy)
                last.then_inc(kt_done, 1)

            def raw_out(n, k):
                act.wait_ge(qkv_full, n + 1)
                at_least(act, rot_done, n - 1)
                at_least(act, v_done, n - 1)
                nc.scalar.activation(raw[:, k % 2, :], pj[:, 0:QKV], ACT.Copy).then_inc(raw_done, 1)

            def probs_out(n, g):
                act.wait_ge(pt_full, WKV * n + g + 1)
                at_least(act, y_full, WKV * (n - 1) + g + 1)
                nc.scalar.activation(pt[:, g, :, :].rearrange("p c n -> p (c n)"), wide[:, :], ACT.Copy
                                     ).then_inc(pt_done, 1)

            def exponential(n, g):
                act.wait_ge(top_done, WKV * n + g + 1)
                at_least(act, pt_full, WKV * (n - 1) + g + 1)
                for s in range(NC * PAIRS):
                    last = nc.scalar.activation(pr[:, g, s, :], sc[g][:, s * P:(s + 1) * P], ACT.Exp,
                                                bias=minus_top[:, g, s:s + 1])
                last.then_inc(exp_done, 1)

            def output_high(n):
                act.wait_ge(yt_full, C0 + n + 1)
                act.wait_ge(wo_full, C0 + n)
                nc.scalar.activation(yt_hi[:, :, :, :].rearrange("p a c n -> p c a n"),
                                     tr[:, 0:D].rearrange("p (c a n) -> p c a n", c=NC, a=2), ACT.Copy
                                     ).then_inc(yt_hi_done, 1)

            def input_high(n, k):
                act.wait_ge(tp_full, n + 1)
                at_least(act, qkv_full, n - 1)
                nc.scalar.activation(xt_hi[:, k % 2, :, :], tr[:, 0:D].rearrange("p (j t) -> p j t", j=KD), ACT.Copy
                                     ).then_inc(xt_hi_done, 1)

            def body(i):
                for k in range(U):
                    n = U * i + k
                    if live(n - 2, NT):
                        keys_out(n - 2, k - 2)
                    if live(n - 3, NT):
                        probs_out(n - 3, 0)
                    if live(n - 1, NT):
                        raw_out(n - 1, k - 1)
                    if live(n - 3, NT):
                        exponential(n - 3, 3)
                    if live(n - 3, NT):
                        probs_out(n - 3, 1)
                    if live(n - 3, NT):
                        probs_out(n - 3, 2)
                    if live(n - 2, NT):
                        exponential(n - 2, 0)
                    if live(n - 4, NT):
                        output_high(n - 4)
                    if live(n - 3, NT):
                        probs_out(n - 3, 3)
                    if live(n - 2, NT):
                        exponential(n - 2, 1)
                    if live(n, NT):
                        input_high(n, k)
                    if live(n - 1, NT):
                        queries_out(n - 1, k - 1)
                    if live(n - 2, NT):
                        exponential(n - 2, 2)

            skewed(act, body, N, first=2)

        @block.tensor
        def _(pe):
            pe.wait_ge(consts_set, 6)
            pe.wait_ge(masks_set, 2)
            pe.sem_inc(wo_full, C0)
            pe.sem_inc(yt_full, C0)

            def transposes(n, k):
                pe.wait_ge(xn_done, n + 1)
                at_least(pe, yt_ready, C0 + n - 3)
                at_least(pe, kt_done, n - 1)
                for j in range(KD):
                    last = nc.tensor.transpose(tr[:, j * P:(j + 1) * P], xn[:, k % 2, j * P:(j + 1) * P],
                                               ident[:, :])
                last.then_inc(tp_full, 1)

            def three(out, x, w):
                todo = [(j, a, b) for j in range(KD) for a, b in ((0, 0), (0, 1), (1, 0))]
                for m, (j, a, b) in enumerate(todo):
                    last = nc.tensor.matmul(out, x(a, j), w(b, j), start=(m == 0), stop=(m == len(todo) - 1))
                return last

            def project(n, k):
                pe.wait_ge(xt_ready, n + 1)
                at_least(pe, wo_done, C0 + n - 3)
                xs = (xt_hi, xt_lo)
                three(pj[:, 0:QKV], lambda a, j: xs[a][:, k % 2, j, :], lambda b, j: qkv[b][:, j, :]
                      ).then_inc(qkv_full, 1)

            def transpose_queries(n, k, m):
                at_least(pe, pt_done, WKV * (m - 2))
                pe.wait_ge(padded_done, n + 1)
                cols = wide[:, :].rearrange("p (u c a n) -> p u a c n", u=PAIRS, c=NC, a=2)
                for ua in range(2 * PAIRS):
                    last = nc.tensor.transpose(cols[:, ua // 2, ua % 2, :, :],
                                               padded[:, k % 2, ua, :, :].rearrange("p g d -> p (g d)"),
                                               ident[:, :])
                last.then_inc(tq_full, 1)

            def transpose_keys(n, k, m):
                if live(m - 1, NT):
                    at_least(pe, xt_ready, m)
                else:
                    pe.wait_ge(yt_ready, C0 + m - 4)
                nc.tensor.transpose(tr[:, 0:P], padded[:, k % 2, 2 * PAIRS, :, :].rearrange("p g d -> p (g d)"),
                                    ident[:, :]).then_inc(tk_full, 1)

            def scores(n, k, g):
                if g == 0:
                    pe.wait_ge(qt_done, n + 1)
                    pe.wait_ge(kt_moved, n + 1)
                at_least(pe, exp_done, WKV * (n - 1) + g + 1)
                first = isinstance(n, int) and n < B
                nc.tensor.matmul(sc[g][:, :], ident_b[:, :], masks[:, 0 if first else 1, :], start=True, stop=False)
                for ch in range(NC):
                    keys = kt[:, k % R, g, 2 * (1 - ch):2 * (1 - ch) + 2, :].rearrange("p s m -> p (s m)")
                    for u in range(PAIRS):
                        col = (ch * PAIRS + u) * P
                        last = nc.tensor.matmul(sc[g][:, col:col + P],
                                                qt[:, k % 2, u, ch, :], keys,
                                                start=False, stop=(ch == NC - 1 and u == PAIRS - 1))
                last.then_inc(sc_full, 1)

            def transpose_probs(n, g, m):
                pe.wait_ge(exp_done, WKV * n + g + 1)
                if g == 0:
                    if live(m - 2, NT):
                        pe.wait_ge(qt_done, m - 1)
                    else:
                        pe.wait_ge(pt_done, WKV * n)
                else:
                    pe.wait_ge(pt_done, WKV * n + g)
                for s in range(NC * PAIRS):
                    last = nc.tensor.transpose(wide[:, s * P:(s + 1) * P], pr[:, g, s, :], ident[:, :])
                last.then_inc(pt_full, 1)

            def weighted(n, k, g):
                pe.wait_ge(pt_done, WKV * n + g + 1)
                pe.wait_ge(v_done, n + 1)
                if g == 0:
                    at_least(pe, yn_done, n)
                for ch, v in enumerate((v_even, v_odd)):
                    for u in range(PAIRS):
                        col = ((ch * PAIRS + u) * WKV + g) * (WD + 1)
                        last = nc.tensor.matmul(yp[:, col:col + WD + 1], pt[:, g, ch * PAIRS + u, :],
                                                v[:, k % R, g, :], start=True, stop=True)
                last.then_inc(y_full, 1)

            def transpose_outputs(n, m):
                pe.wait_ge(yn_done, n + 1)
                if live(m - 2, NT):
                    pe.wait_ge(kt_done, m - 1)
                else:
                    pe.wait_ge(yt_ready, C0 + n)
                for ch in range(NC):
                    last = nc.tensor.transpose(tr[:, ch * P:(ch + 1) * P], yn[:, ch, :], ident[:, :])
                last.then_inc(yt_full, 1)

            def out_product(n, m):
                pe.wait_ge(yt_ready, C0 + n + 1)
                if live(m - 1, NT):
                    pe.wait_ge(raw_done, m)
                else:
                    pe.wait_ge(wo_done, C0 + n)
                ys = (yt_hi, yt_lo)
                three(pj[:, 0:D], lambda a, j: ys[a][:, j, :, :].rearrange("p c n -> p (c n)"),
                      lambda b, j: out_w[b][:, j, :]).then_inc(wo_full, 1)

            def body(i):
                for k in range(U):
                    n = U * i + k
                    one, two, three_, four = (live(n - lag, NT) for lag in (1, 2, 3, 4))
                    if two:
                        transpose_keys(n - 2, k - 2, n)
                    if three_:
                        transpose_probs(n - 3, 0, n)
                    if one:
                        project(n - 1, k - 1)
                    if three_:
                        weighted(n - 3, k - 3, 0)
                        transpose_probs(n - 3, 1, n)
                    if two:
                        scores(n - 2, k - 2, 0)
                    if three_:
                        transpose_probs(n - 3, 2, n)
                        weighted(n - 3, k - 3, 1)
                    if two:
                        scores(n - 2, k - 2, 1)
                    if four:
                        transpose_outputs(n - 4, n)
                    if three_:
                        transpose_probs(n - 3, 3, n)
                        weighted(n - 3, k - 3, 2)
                    if two:
                        scores(n - 2, k - 2, 2)
                    if live(n, NT):
                        transposes(n, k)
                    if three_:
                        weighted(n - 3, k - 3, 3)
                    if one:
                        transpose_queries(n - 1, k - 1, n)
                    if two:
                        scores(n - 2, k - 2, 3)
                    if four:
                        out_product(n - 4, n)

            skewed(pe, body, N)


def hybrid_block(nc, d, out):
    x_blocks = d["x"].rearrange("(b q) d -> b q d", q=BT)
    out_blocks = out.rearrange("(b q) d -> b q d", q=BT)
    with ExitStack() as ctx:
        def sb(n, shape, dt=F32, at=ctx):
            return at.enter_context(nc.sbuf_tensor(n, shape, dt))

        def pair(n, shape, at):
            return [sb(f"{n}_{half}", shape, F32R, at) for half in ("hi", "lo")]

        def whole(t):
            return t[tuple(slice(None) for _ in t.shape)]

        X = sb("X", [P, NT, D])
        staging = sb("staging", [P, 2 * KD * FF])
        kept = {n: sb(f"c_{n}", list(d[n].shape)) for n in ("ident", "ln1", "ln2", "gn", "b1", "b2")}
        ident = kept["ident"]

        def staged(weights):
            out_, at = [], 0
            for w in weights:
                rows, n = w.shape
                size = rows // P * n
                out_.append((staging[:, at:at + size].rearrange("p (k n) -> p k n", n=n),
                             w.rearrange("(k p) n -> p k n", p=P)))
                at += size
            return out_

        ret_stages = [staged([d[n][layer] for n in ("wqkv", "wg", "wo")]) for layer in range(L)]
        ffn_stages = [staged([d[n][layer] for n in ("w1", "w2")]) for layer in range(L)]
        ternary_stages = staged([d["w_up"], d["w_down"]])

        win_stage, at = {}, 0
        for n in ("win_wqkv", "win_wo", "pair_mix", "q_gain", "win_rotary", "win_masks"):
            src = d[n].rearrange("(k p) n -> p k n", p=P) if n == "win_wqkv" else d[n]
            size = int(np.prod(src.shape[1:]))
            view = staging[:, at:at + size]
            names = "abcd"[:len(src.shape) - 1]
            if len(names) > 1:
                view = view.rearrange(f"p ({' '.join(names)}) -> p {' '.join(names)}",
                                      **dict(zip(names[1:], src.shape[2:])))
            win_stage[n] = (view, src)
            at += size + (WKV if n == "q_gain" else 0)

        tables_at = ctx.enter_context(ExitStack())
        tabs = {n: sb(n, list(d[n].shape), at=tables_at)
                for n in ("rotary", "decay", "state_decay", "causal", "heads")}
        with nc.cleanup_on_exit():
            input_norm(nc, X, d["x"], ret_stages[0] + [(whole(t), d[n]) for n, t in (*kept.items(), *tabs.items())])
        for layer in range(L):
            with ExitStack() as c:
                qkv = pair(f"qkv{layer}", [P, KD, 3 * D], c)
                gate = pair(f"gate{layer}", [P, KD, D], c)
                out_w = pair(f"out_w{layer}", [P, KD, D], c)
                jobs = [(*stage, *w) for stage, w in zip(ret_stages[layer], (qkv, gate, out_w))]
                with nc.cleanup_on_exit():
                    retention(nc, f"ret{layer}", X, ident, qkv=qkv, gate=gate, out_w=out_w,
                              norm=kept["ln1"][:, layer], gn=kept["gn"][:, layer],
                              loads=ffn_stages[layer], jobs=jobs, **tabs)
            if layer == L - 1:
                tables_at.close()
            with ExitStack() as c:
                up = pair(f"up{layer}", [P, KD, FF], c)
                down = pair(f"down{layer}", [P, MF, D], c)
                with nc.cleanup_on_exit():
                    ffn(nc, f"ffn{layer}", X, ident, up=up, down=down, norm=kept["ln2"][:, layer],
                        hidden_bias=kept["b1"][:, layer], out_bias=kept["b2"][:, layer],
                        first_input=x_blocks if layer == L - 1 else None,
                        loads=ternary_stages if layer == L - 1 else ret_stages[layer + 1],
                        jobs=[(*stage, *w) for stage, w in zip(ffn_stages[layer], (up, down))])

        up_t = sb("up_ternary", [P, KD, FF], F32R)
        down_t = sb("down_ternary", [P, MF, D], F32R)
        with nc.cleanup_on_exit():
            ternary_weights(nc, "ternary", [(ternary_stages[0][0], up_t), (ternary_stages[1][0], down_t)])
        with nc.cleanup_on_exit():
            ffn(nc, "ternary_ffn0", X, ident, up=(up_t,), down=(down_t,), loads=list(win_stage.values()))

        with ExitStack() as c:
            qkv = pair("win_qkv", [P, KD, (WH + 2 * WKV) * WD], c)
            out_w = pair("win_out", [P, 2, D], c)
            first = sum(int(np.prod(win_stage[n][1].shape[1:])) for n in ("win_wqkv", "win_wo", "pair_mix"))
            gain = staging[:, first:first + WH + WKV]
            with nc.cleanup_on_exit():
                window_weights(nc, "win_mix", win_stage["win_wo"][0], win_stage["pair_mix"][0], *out_w, gain,
                               [(*win_stage["win_wqkv"], *qkv)])
            with nc.cleanup_on_exit():
                window_attention(nc, "wa", X, ident, qkv=qkv, out_w=out_w, gain=gain,
                                 win_rotary=win_stage["win_rotary"][0], win_masks=win_stage["win_masks"][0])

        with nc.cleanup_on_exit():
            ffn(nc, "ternary_ffn1", X, ident, up=(up_t,), down=(down_t,), out_dram=out_blocks)


def lay_out(i):
    def get(n):
        return np.asarray(i[n])

    def a(n):
        return get(f"L0_attn_a_{n}")

    def heads_in_columns(w):
        return w.transpose(0, 2, 1, 3).reshape(L, D, D)

    def on_partitions(w, b):
        return np.stack([w, b], 1).reshape(L, 2, KD, P).transpose(3, 0, 1, 2)

    def head_rows(w):
        return w.reshape(WKV, PAIRS, 2, WD, -1).transpose(1, 2, 0, 3, 4).reshape(w.shape)

    b = "L0_attn_b_"
    mix = get(b + "pair_mix").reshape(WKV, PAIRS, 2, 2).transpose(1, 0, 2, 3)[:, :, None]
    return dict(
        x=a("X").reshape(T, D),
        ln1=on_partitions(a("ln1_w"), a("ln1_b")),
        ln2=on_partitions(a("ln2_w"), a("ln2_b")),
        gn=on_partitions(a("gn_w"), a("gn_b")),
        b1=a("ffn_b1").reshape(L, MF, P).transpose(2, 0, 1),
        b2=np.broadcast_to(a("ffn_b2"), (P, L, D)),
        wqkv=np.concatenate([heads_in_columns(a(n)) for n in ("WQ", "WK", "WV")], 2),
        wg=a("WG"), wo=a("WO"), w1=a("ffn_w1"), w2=a("ffn_w2"),
        w_up=get("L0_ffn_w_up").T, w_down=get("L0_ffn_w_down").T,
        win_wqkv=np.concatenate([head_rows(get(b + "Wq")), get(b + "Wk"), get(b + "Wv")], 0).T,
        win_wo=get(b + "Wo").T.reshape(WKV, PAIRS, 2, WD, D).transpose(1, 0, 3, 2, 4).reshape(P, 2, D),
        pair_mix=np.broadcast_to(mix, (PAIRS, WKV, WD, 2, 2)).reshape(P, 2, 2),
        q_gain=np.broadcast_to(get(b + "q_gain").reshape(WKV, PAIRS, 2).transpose(1, 2, 0).reshape(WH), (P, WH)),
        ident=np.eye(P, dtype=np.float32),
        **retention_tables(), **window_tables())


def kernel(**inputs):
    import concourse.bacc as bacc
    from concourse.bass_utils import run_bass_kernel_spmd

    nc = bacc.Bacc("TRN2", target_bir_lowering=False, num_devices=1)
    arrays, dram = {}, {}
    for name, a in lay_out(inputs).items():
        arrays[f"in_{name}"] = np.ascontiguousarray(a)
        dram[name] = nc.dram_tensor(f"in_{name}", a.shape, F32, kind="ExternalInput").ap()
    out = nc.dram_tensor("out_0", [T, D], F32, kind="ExternalOutput").ap()
    hybrid_block(nc, dram, out)
    results = run_bass_kernel_spmd(nc, [arrays], core_ids=[0]).results
    return results[0]["out_0"].reshape(B, S, D)
```
